# Optimizing a Trainium2 kernel written in Bass

```python
import numpy as np
import jax
import jax.numpy as jnp

def _softmax(x, axis=-1):
    return jax.nn.softmax(x, axis=axis)

def _gelu(x):
    return jax.nn.gelu(x, approximate=True)

def _silu(x):
    return jax.nn.silu(x)

def _sigmoid(x):
    return jax.nn.sigmoid(x)

def _layernorm(x, axis=-1, eps=1e-05):
    m = jnp.mean(x, axis=axis, keepdims=True)
    v = jnp.var(x, axis=axis, keepdims=True)
    return (x - m) / jnp.sqrt(v + eps)

def _scatter_add(tgt, idx, src, axis=0):
    return tgt.at[idx].add(src)

def _segment_sum(src, seg, n):
    return jax.ops.segment_sum(src, seg, n)
kernel_name = 'mk_conv_attn_hybrid_d2_conv_nhwc768_r4_7c8586'

def setup_inputs(seed: int=0):
    np.random.seed(seed)
    _w = jnp.asarray

    def _rec_inputs():
        import jax
        import jax.numpy as jnp
        _gk = jax.random.key(seed)
        x = -4.65e-05 + 0.9999 * jax.random.normal(jax.random.fold_in(_gk, 1), (16, 16, 16, 192), jnp.float32)
        return x
    x = _rec_inputs()

    def _L0_conv_setup():
        import jax, jax.numpy as jnp
        import numpy as np
        P = 3

        def dct_basis(n, dtype):
            k = jnp.arange(n, dtype=dtype)[:, None]
            i = jnp.arange(n, dtype=dtype)[None, :]
            C = jnp.cos(jnp.pi / n * (i + 0.5) * k)
            scale = jnp.where(k == 0, 1.0 / np.sqrt(n), np.sqrt(2.0 / n)).astype(dtype)
            return C * scale
        key = jax.random.key(seed)
        kf, kw = jax.random.split(key)
        B, H, W, D = (16, 16, 16, 192)
        f = jax.random.normal(kf, (B, H, W, D), dtype=jnp.float32)
        W1 = jax.random.normal(kw, (D, D), dtype=jnp.float32) * 0.02
        b1 = jnp.zeros((D,), dtype=jnp.float32)
        return {'f': f, 'W1': W1, 'b1': b1}
    _L0_conv_all = _L0_conv_setup()
    _L0_conv_in = {k: v for k, v in _L0_conv_all.items() if k in ('W1', 'b1')}
    del _L0_conv_all

    def _L1_attn_setup():
        import jax, jax.numpy as jnp
        import numpy as np
        EPS = 1e-05

        def _layernorm(x, w, b):
            mu = jnp.mean(x, axis=-1, keepdims=True)
            var = jnp.mean(jnp.square(x - mu), axis=-1, keepdims=True)
            return (x - mu) * jax.lax.rsqrt(var + EPS) * w + b
        key = jax.random.key(seed)
        ks = jax.random.split(key, 8)
        B, S, D = (4, 512, 192)
        H = int(2.0 * D)
        QK = 32
        s = lambda fan_in: 1.0 / np.sqrt(fan_in)
        return {'x': jax.random.normal(ks[0], (B, S, D), dtype=jnp.float32), 'ln_w': jnp.ones((D,), jnp.float32), 'ln_b': jnp.zeros((D,), jnp.float32), 'W_hidden': jax.random.normal(ks[1], (H * 2, D), jnp.float32) * s(D), 'b_hidden': jnp.zeros((H * 2,), jnp.float32), 'W_qk': jax.random.normal(ks[2], (QK, D), jnp.float32) * s(D), 'b_qk': jnp.zeros((QK,), jnp.float32), 'gamma': jax.random.normal(ks[3], (2, QK), jnp.float32) * 0.02, 'beta': jnp.zeros((2, QK), jnp.float32), 'W_out': jax.random.normal(ks[4], (D, H), jnp.float32) * s(H), 'b_out': jnp.zeros((D,), jnp.float32)}
    _L1_attn_all = _L1_attn_setup()
    _L1_attn_in = {k: v for k, v in _L1_attn_all.items() if k in ('ln_w', 'ln_b', 'W_hidden', 'b_hidden', 'W_qk', 'b_qk', 'gamma', 'beta', 'W_out', 'b_out')}
    del _L1_attn_all

    def _L1_ffn_setup():
        import jax, jax.numpy as jnp
        import numpy as np
        B, S, H, F, E, TOP_K = (4, 512, 192, 768, 8, 2)
        key = jax.random.key(seed)
        ks = jax.random.split(key, 6)
        x = jax.random.normal(ks[0], (B, S, H), dtype=jnp.float32)
        Wr = jax.random.normal(ks[1], (E, H), dtype=jnp.float32) * 0.02
        Wi = jax.random.normal(ks[2], (E, F, H), dtype=jnp.float32) * 0.02
        bi = jnp.zeros((E, F), dtype=jnp.float32)
        Wo = jax.random.normal(ks[3], (E, H, F), dtype=jnp.float32) * 0.02
        bo = jnp.zeros((E, H), dtype=jnp.float32)
        return {'x': x, 'Wr': Wr, 'Wi': Wi, 'bi': bi, 'Wo': Wo, 'bo': bo}
    _L1_ffn_all = _L1_ffn_setup()
    _L1_ffn_in = {k: v for k, v in _L1_ffn_all.items() if k in ('Wr', 'Wi', 'bi', 'Wo', 'bo')}
    del _L1_ffn_all
    return {'x': x, 'L0_conv_W1': _L0_conv_in['W1'], 'L0_conv_b1': _L0_conv_in['b1'], 'L1_attn_ln_w': _L1_attn_in['ln_w'], 'L1_attn_ln_b': _L1_attn_in['ln_b'], 'L1_attn_W_hidden': _L1_attn_in['W_hidden'], 'L1_attn_b_hidden': _L1_attn_in['b_hidden'], 'L1_attn_W_qk': _L1_attn_in['W_qk'], 'L1_attn_b_qk': _L1_attn_in['b_qk'], 'L1_attn_gamma': _L1_attn_in['gamma'], 'L1_attn_beta': _L1_attn_in['beta'], 'L1_attn_W_out': _L1_attn_in['W_out'], 'L1_attn_b_out': _L1_attn_in['b_out'], 'L1_ffn_Wr': _L1_ffn_in['Wr'], 'L1_ffn_Wi': _L1_ffn_in['Wi'], 'L1_ffn_bi': _L1_ffn_in['bi'], 'L1_ffn_Wo': _L1_ffn_in['Wo'], 'L1_ffn_bo': _L1_ffn_in['bo']}

def reference(x, L0_conv_W1, L0_conv_b1, L1_attn_ln_w, L1_attn_ln_b, L1_attn_W_hidden, L1_attn_b_hidden, L1_attn_W_qk, L1_attn_b_qk, L1_attn_gamma, L1_attn_beta, L1_attn_W_out, L1_attn_b_out, L1_ffn_Wr, L1_ffn_Wi, L1_ffn_bi, L1_ffn_Wo, L1_ffn_bo):
    import jax
    import jax.numpy as jnp

    def _L0_conv_ref(f, W1, b1):
        import jax, jax.numpy as jnp
        import numpy as np
        P = 3

        def dct_basis(n, dtype):
            k = jnp.arange(n, dtype=dtype)[:, None]
            i = jnp.arange(n, dtype=dtype)[None, :]
            C = jnp.cos(jnp.pi / n * (i + 0.5) * k)
            scale = jnp.where(k == 0, 1.0 / np.sqrt(n), np.sqrt(2.0 / n)).astype(dtype)
            return C * scale
        B, H, W, D = f.shape
        Hp = (H + P - 1) // P * P
        Wp = (W + P - 1) // P * P
        if Hp != H or Wp != W:
            f = jnp.pad(f, ((0, 0), (0, Hp - H), (0, Wp - W), (0, 0)), mode='edge')
        C = dct_basis(P, f.dtype)
        x = f.reshape(B, Hp // P, P, Wp // P, P, D).transpose(0, 1, 3, 2, 4, 5)
        x = jnp.einsum('ap,bhwpqd->bhwaqd', C, x)
        x = jnp.einsum('bhwaqd,cq->bhwacd', x, C)
        x = jax.nn.gelu(jnp.einsum('...i,oi->...o', x, W1) + b1, approximate=False)
        x = jnp.einsum('pa,bhwpqd->bhwaqd', C, x)
        x = jnp.einsum('bhwaqd,qc->bhwacd', x, C)
        out = x.transpose(0, 1, 3, 2, 4, 5).reshape(B, Hp, Wp, D)
        return out[:, :H, :W, :]

    def _L1_attn_ref(x, ln_w, ln_b, W_hidden, b_hidden, W_qk, b_qk, gamma, beta, W_out, b_out):
        import jax, jax.numpy as jnp
        import numpy as np
        EPS = 1e-05

        def _layernorm(x, w, b):
            mu = jnp.mean(x, axis=-1, keepdims=True)
            var = jnp.mean(jnp.square(x - mu), axis=-1, keepdims=True)
            return (x - mu) * jax.lax.rsqrt(var + EPS) * w + b
        seq_len = x.shape[-2]
        normed = _layernorm(x, ln_w, ln_b)
        hg = jax.nn.silu(jnp.einsum('bsd,hd->bsh', normed, W_hidden) + b_hidden)
        v, gate = jnp.split(hg, 2, axis=-1)
        Z = jax.nn.silu(jnp.einsum('bsd,qd->bsq', normed, W_qk) + b_qk)
        q = Z * gamma[0] + beta[0]
        k = Z * gamma[1] + beta[1]
        sim = jnp.einsum('bid,bjd->bij', q, k) / seq_len
        A = jnp.square(jax.nn.relu(sim))
        V = jnp.einsum('bij,bjd->bid', A, v) * gate
        out = jnp.einsum('bih,dh->bid', V, W_out) + b_out
        return out + x

    def _L1_ffn_ref(x, Wr, Wi, bi, Wo, bo):
        import jax, jax.numpy as jnp
        import numpy as np
        B, S, H, F, E, TOP_K = (4, 512, 192, 768, 8, 2)
        xf = x.reshape(-1, x.shape[-1])
        router_logits = jnp.einsum('th,eh->te', xf, Wr)
        topk_vals, topk_idx = jax.lax.top_k(router_logits, TOP_K)
        routing_weights = jax.nn.softmax(topk_vals, axis=-1)
        h = jnp.einsum('th,efh->etf', xf, Wi) + bi[:, None, :]
        h = jax.nn.gelu(h, approximate=False)
        expert_out = jnp.einsum('etf,ehf->eth', h, Wo) + bo[:, None, :]
        expert_out = jnp.transpose(expert_out, (1, 0, 2))
        gathered = jnp.take_along_axis(expert_out, topk_idx[:, :, None], axis=1)
        out = jnp.einsum('tk,tkh->th', routing_weights, gathered)
        return out.reshape(x.shape)

    def _gn(v, G=32, eps=1e-05):
        B_, H_, W_, C_ = v.shape
        g = v.reshape(B_, H_, W_, G, C_ // G)
        m = jnp.mean(g, axis=(1, 2, 4), keepdims=True)
        s = jnp.var(g, axis=(1, 2, 4), keepdims=True)
        return ((g - m) / jnp.sqrt(s + eps)).reshape(v.shape)

    def _ln_c(v, eps=1e-06):
        m = jnp.mean(v, axis=-1, keepdims=True)
        s = jnp.var(v, axis=-1, keepdims=True)
        return (v - m) / jnp.sqrt(s + eps)

    def _ln_t(v, eps=1e-05):
        m = jnp.mean(v, axis=-1, keepdims=True)
        s = jnp.var(v, axis=-1, keepdims=True)
        return (v - m) / jnp.sqrt(s + eps)

    def _to_tokens(v):
        B_, H_, W_, C_ = v.shape
        return v.reshape(B_, H_ * W_, C_)

    def _from_tokens(t, like):
        return t.reshape(like.shape)
    x = x + _L0_conv_ref(_gn(x), L0_conv_W1, L0_conv_b1)
    t = _to_tokens(x)
    t = t + _L1_attn_ref(_ln_t(t), L1_attn_ln_w, L1_attn_ln_b, L1_attn_W_hidden, L1_attn_b_hidden, L1_attn_W_qk, L1_attn_b_qk, L1_attn_gamma, L1_attn_beta, L1_attn_W_out, L1_attn_b_out)
    t = t + _L1_ffn_ref(_ln_t(t), L1_ffn_Wr, L1_ffn_Wi, L1_ffn_bi, L1_ffn_Wo, L1_ffn_bo)
    x = _from_tokens(t, x)
    return x

_drawn_inputs = setup_inputs


def setup_inputs(seed=0):
    import zlib

    import numpy as np

    out = dict(_drawn_inputs(seed))
    spreads = {'L0_conv_b1': (0.0, 0.1),
     'L1_attn_ln_w': (1.0, 0.6),
     'L1_attn_ln_b': (0.0, 0.8),
     'L1_attn_b_hidden': (0.0, 0.8),
     'L1_attn_b_qk': (0.0, 0.8),
     'L1_attn_beta': (0.0, 0.8),
     'L1_attn_b_out': (0.0, 2.0),
     'L1_ffn_bi': (0.0, 2.0),
     'L1_ffn_bo': (0.0, 2.0)}
    factors = {'L1_attn_W_hidden': 8.0,
     'L1_attn_W_qk': 8.0,
     'L1_attn_gamma': 8.0,
     'L1_attn_W_out': 8.0,
     'L1_ffn_Wr': 28.674,
     'L1_ffn_Wi': 37.293,
     'L1_ffn_Wo': 24.685}
    for name, (base, spread) in spreads.items():
        noise = np.random.default_rng([zlib.crc32(name.encode()), seed]).standard_normal(out[name].shape)
        drawn = base * np.exp(spread * noise) if base else spread * noise
        out[name] = jnp.asarray(drawn.astype(out[name].dtype))
    for name, factor in factors.items():
        out[name] = (out[name] * factor).astype(out[name].dtype)
    return out
```

```python
from contextlib import ExitStack

import numpy as np
import concourse.bass as bass
from concourse import mybir

IMAGES, SIDE, D = 16, 16, 192
TOKENS = IMAGES * SIDE * SIDE
SEQ = SIDE * SIDE
P = 128
HALVES = SEQ // P
GROUPS = 32
GC = D // GROUPS
BLOCK = 3
BROWS = -(-SIDE // BLOCK)
FCH = 2 * BROWS * BLOCK * BLOCK
NFC = BROWS // 2
KC = 96
NKC = D // KC
HID = 2 * D
QK = 32
EXPERTS, FF = 8, 768
FCHUNKS = FF // P
REGION = TOKENS + P
SPARE = EXPERTS * REGION
ROW = D + 2
MOE_TILES = (2 * TOKENS + EXPERTS * (P - 1)) // P
LN_EPS = 1e-5

_WIDTHS = [("ident", P), ("ones", P), ("before", P), ("fwd0", 2 * FCH), ("fwd1", 2 * FCH),
           ("inv0a", P), ("inv0b", P), ("inv1b", P), ("inv1c", P), ("lower", EXPERTS * EXPERTS),
           ("list_base", EXPERTS), ("tile_rows", TOKENS // P), ("tile_no", MOE_TILES), ("ids", HALVES),
           ("pad_id", 1), ("half", GROUPS)]
CONST_AT, CONST_W = {}, 0
for _n, _w in _WIDTHS:
    CONST_AT[_n] = (CONST_W, CONST_W + _w)
    CONST_W += _w


def shape_constants():
    c = np.zeros((P, CONST_W), np.float32)

    def put(name, a):
        lo, _ = CONST_AT[name]
        c[:a.shape[0], lo:lo + a.shape[1]] = a

    k, n = np.arange(BLOCK)[:, None], np.arange(BLOCK)[None, :]
    dct = np.cos(np.pi / BLOCK * (n + 0.5) * k) * np.where(k == 0, np.sqrt(1 / BLOCK), np.sqrt(2 / BLOCK))
    fwd = np.zeros((SEQ, NFC * FCH))
    inv = np.zeros((NFC * FCH, SEQ))
    for bh in range(BROWS):
        for bw in range(BROWS):
            for a in range(BLOCK):
                for b in range(BLOCK):
                    f = ((bh * BROWS + bw) * BLOCK + a) * BLOCK + b
                    for r in range(BLOCK):
                        for s in range(BLOCK):
                            h, w = bh * BLOCK + r, bw * BLOCK + s
                            fwd[min(h, SIDE - 1) * SIDE + min(w, SIDE - 1), f] += dct[a, r] * dct[b, s]
                            if h < SIDE and w < SIDE:
                                inv[f, h * SIDE + w] = dct[a, r] * dct[b, s]
    assert not fwd[:P, 2 * FCH:].any() and not fwd[P:, :FCH].any()
    put("ident", np.eye(P))
    put("ones", np.ones((P, P)))
    put("before", np.triu(np.ones((P, P)), 1))
    put("fwd0", fwd[:P, :2 * FCH])
    put("fwd1", fwd[P:, FCH:])
    put("inv0a", inv[:FCH, :P])
    put("inv0b", inv[FCH:2 * FCH, :P])
    put("inv1b", inv[FCH:2 * FCH, P:])
    put("inv1c", inv[2 * FCH:, P:])
    assert not inv[:FCH, P:].any() and not inv[2 * FCH:, :P].any()
    every = np.ones((P, 1))
    put("lower", every * np.tril(np.ones((EXPERTS, EXPERTS)), -1).reshape(1, -1))
    put("list_base", every * (np.arange(EXPERTS) * REGION)[None])
    put("tile_rows", every * (np.arange(TOKENS // P) * P)[None])
    put("tile_no", every * np.arange(MOE_TILES)[None])
    put("ids", np.arange(P)[:, None] + P * np.arange(HALVES)[None] - SEQ)
    put("pad_id", TOKENS + np.arange(P)[:, None])
    put("half", np.full((P, GROUPS), -0.5))
    return c


def wait(eng, sem, value):
    if isinstance(value, int) and value <= 0:
        return
    eng.wait_ge(sem, value)


def wait_alone(eng, sem, value, held):
    eng.wait_ge(held, 16)
    eng.wait_ge(sem, value)


class Chain:

    def __init__(self, eng, sem):
        self.eng, self.sem, self.count, self.extra = eng, sem, 0, 0

    def link(self, ins):
        ins.then_inc(self.sem, 1)
        self.count += 1
        self.eng.wait_ge(self.sem, self.count + self.extra)


def pipeline(eng, step, first, last, ahead, behind, chain=None, per=0):
    n = last + 1 - behind
    lo, hi = behind + 1, n - ahead
    for i in range(first, lo):
        step(i)
    with eng.Fori(lo, hi) as i:
        if chain:
            start = chain.count
            chain.extra = (i - lo) * per
        step(i)
    if chain:
        assert chain.count - start == per, (chain.count - start, per)
        chain.count = start + per * (hi - lo)
        chain.extra = 0
    for i in range(hi, last + 1):
        step(i)


def build(nc, x, consts, w1, b1, ln_w, ln_b, w_hid, b_hid, w_qk, b_qk, gamma, beta, w_out, b_out,
          w_r, w_i, b_i, w_o, b_o, out):
    f32, i32 = mybir.dt.float32, mybir.dt.int32
    ALU, ACT, AX = mybir.AluOpType, mybir.ActivationFunctionType, mybir.AxisListType
    ds = bass.ds

    lists = nc.dram_tensor("lists", (SPARE + P, ROW), f32, kind="Internal").ap()

    ctx = ExitStack()
    with ctx:
        def sb(name, shape, dt=f32):
            return ctx.enter_context(nc.sbuf_tensor(name, shape, dt))

        def sem(name):
            return ctx.enter_context(nc.semaphore(name))

        const = sb("const", [P, CONST_W])

        def K(name, rows=P):
            lo, hi = CONST_AT[name]
            return const[0:rows, lo:hi]

        X = sb("X", [P, IMAGES * HALVES, D])
        moments = sb("moments", [P, IMAGES * HALVES, 2])

        w1_sb = sb("w1_sb", [KC + 1, NKC, D])
        gsum = sb("gsum", [P, GROUPS])
        gsq = sb("gsq", [P, GROUPS])
        gmean = sb("gmean", [P, GROUPS])
        gvar = sb("gvar", [P, GROUPS])
        grs = sb("grs", [P, GROUPS])
        xc = sb("xc", [P, HALVES, D])
        xsq = sb("xsq", [P, HALVES, D])
        xn = sb("xn", [P, HALVES, D])
        coef = sb("coef", [KC + 1, NKC, NFC * FCH])
        mixed = sb("mixed", [FCH, NFC, D])
        stats = sb("stats", [P, HALVES, 6])
        mom = sb("mom", [P, HALVES, 2])

        w_hid_sb = sb("w_hid_sb", [KC + 1, NKC, 2 * HID])
        w_qk_sb = sb("w_qk_sb", [KC + 1, NKC, QK])
        w_out_sb = sb("w_out_sb", [P, HID // P, D])
        ln_sb = sb("ln_sb", [KC, 2, NKC])
        gb_sb = sb("gb_sb", [QK, 4])
        b_out_sb = sb("b_out_sb", [P, D])
        w_r_sb = sb("w_r_sb", [KC, NKC, EXPERTS])
        rs1 = sb("rs1", [P, IMAGES * HALVES])
        tmp32 = sb("tmp32", [P, IMAGES * HALVES])
        n_scale = sb("n_scale", [P, IMAGES * HALVES])
        n_bias = sb("n_bias", [P, IMAGES * HALVES])
        r_scale = sb("r_scale", [P, IMAGES * HALVES])
        r_bias = sb("r_bias", [P, IMAGES * HALVES])
        eps_sb = sb("eps_sb", [P, 1])
        normed = sb("normed", [P, HALVES, D])
        nT = sb("nT", [KC + 1, NKC, SEQ])
        zT = sb("zT", [QK, SEQ])
        qT = sb("qT", [QK, SEQ])
        kT = sb("kT", [QK, SEQ])
        v_sb = sb("v_sb", [P, HALVES, HID])
        gateT = sb("gateT", [P, HID // P, SEQ])
        simT = sb("simT", [P, HALVES, SEQ])
        attnT = sb("attnT", [P, HALVES, SEQ])
        gatedT = sb("gatedT", [P, HID // P, SEQ])

        u_var = sb("u_var", [P, HALVES])
        u_scale = sb("u_scale", [P, HALVES])
        u_bias = sb("u_bias", [P, HALVES])
        row_a = sb("row_a", [P, HALVES, ROW])
        row_b = sb("row_b", [P, HALVES, ROW])
        uT = sb("uT", [KC, NKC, SEQ])
        logits = sb("logits", [P, HALVES, EXPERTS])
        above = sb("above", [P, HALVES, EXPERTS, EXPERTS])
        equal = sb("equal", [P, HALVES, EXPERTS, EXPERTS])
        rank = sb("rank", [P, HALVES, EXPERTS])
        chosen = sb("chosen", [P, 2, HALVES * EXPERTS])
        in_row = sb("in_row", [P, EXPERTS])
        in_first = sb("in_first", [P, EXPERTS])
        picked = sb("picked", [P, 2, HALVES * EXPERTS])
        top = sb("top", [P, 2, HALVES])
        diff = sb("diff", [P, HALVES])
        tanh_d = sb("tanh_d", [P, HALVES])
        list_at = sb("list_at", [P, EXPERTS])
        slot = sb("slot", [P, HALVES, EXPERTS])
        slots = sb("slots", [P, 2, HALVES], i32)
        pad_rows = sb("pad_rows", [P, ROW])

        n_list = sb("n_list", [P, EXPERTS])
        over = sb("over", [P, EXPERTS, TOKENS // P])
        n_tiles = sb("n_tiles", [P, EXPERTS])
        t_end = sb("t_end", [P, EXPERTS])
        t_start = sb("t_start", [P, EXPERTS])
        base = sb("base", [P, EXPERTS])
        started = sb("started", [P, MOE_TILES, EXPERTS])
        ended = sb("ended", [P, MOE_TILES, EXPERTS])
        rows_at = sb("rows_at", [P, MOE_TILES, EXPERTS])
        tile_f = sb("tile_f", [P, MOE_TILES])
        tile_expert = sb("tile_expert", [P, MOE_TILES], i32)
        tile_row = sb("tile_row", [P, MOE_TILES], i32)
        list_end = sb("list_end", [P, EXPERTS], i32)

        w_i_sb = sb("w_i_sb", [KC + 1, EXPERTS, NKC, FF])
        w_o_sb = sb("w_o_sb", [P, EXPERTS, FCHUNKS, D])
        b_o_sb = sb("b_o_sb", [P, EXPERTS, D])
        slot_rows = sb("slot_rows", [P, ROW])
        meta = sb("meta", [P, MOE_TILES, 2], i32)
        sT = sb("sT", [KC + 1, NKC, P])
        h_sb = sb("h_sb", [P, FF])
        hT = sb("hT", [P, FF])
        y_sb = sb("y_sb", [P, D])
        y_id = sb("y_id", [P, 1], i32)

        ps = ctx.enter_context(nc.psum_tensor("ps", [P, 8, 512], f32))

        ps_coef = ps[0:KC, 0:2, 0:NFC * FCH]
        ps_mix = ps[:, 2:4, :].rearrange("p b (k c) -> p (b k) c", c=256)[0:FCH, 0:NFC, 0:D]
        ps_conv = ps[:, 4, 0:HALVES * D].rearrange("p (t c) -> p t c", c=D)
        ps_gsum, ps_gsq = ps[:, 5, 0:GROUPS], ps[:, 6, 0:GROUPS]
        ps_nT = ps[0:KC, 0, :].rearrange("p (k n) -> p k n", k=NKC)
        ps_z = ps[0:QK, 1, 0:SEQ]
        ps_sim = ps[:, 1, :].rearrange("p (t n) -> p t n", t=HALVES)
        ps_v = ps[:, 2:4, 0:HID]
        ps_av = ps[:, 2:4, :].rearrange("p b (k n) -> p (b k) n", n=SEQ)[:, 0:HID // P, :]
        ps_gate = ps[:, 4:6, :].rearrange("p b (k n) -> p (b k) n", n=SEQ)[:, 0:HID // P, :]
        ps_out = ps[:, 6, 0:HALVES * D].rearrange("p (t c) -> p t c", c=D)
        ps_uT = ps[0:KC, 7, :].rearrange("p (k n) -> p k n", k=NKC)
        ps_logits = ps[:, 7, 0:HALVES * EXPERTS].rearrange("p (t e) -> p t e", e=EXPERTS)
        ps_rows_before = ps[:, 7, 64:64 + EXPERTS]
        ps_rows_all = ps[:, 7, 128:128 + EXPERTS]
        ps_h = ps[:, 0:2, 0:FF // 2]
        ps_hT = ps[:, 2:4, 0:FF // 2]
        ps_sT = ps[0:KC, 4, 0:NKC * P].rearrange("p (k n) -> p k n", k=NKC)
        ps_y = ps[:, 5, 0:D]

        ld_const, ld_w1, ld_x, ld_attn, ld_exp = (sem(f"ld_{n}") for n in ("const", "w1", "x", "attn", "exp"))
        ones_set = sem("ones_set")
        dve_self, act_self, pool_self = sem("dve_self"), sem("act_self"), sem("pool_self")
        gsum_in, gsum_done = sem("gsum_in"), sem("gsum_done")
        xc_done, sq_done = sem("xc_done"), sem("sq_done")
        gsq_in, gsq_done, gvar_done, xn_done = sem("gsq_in"), sem("gsq_done"), sem("gvar_done"), sem("xn_done")
        coef_ps, coef_done = sem("coef_ps"), sem("coef_done")
        mix_ps, mix_done, conv_ps, conv_read, conv_done = (
            sem(n) for n in ("mix_ps", "mix_done", "conv_ps", "conv_read", "conv_done"))
        mom_var, mom_std, mom2_var, mom2_std, scales_done = (
            sem(n) for n in ("mom_var", "mom_std", "mom2_var", "mom2_std", "scales_done"))
        normed_done, nT_ps, nT_done, z_ps, z_done, qk_done = (
            sem(n) for n in ("normed_done", "nT_ps", "nT_done", "z_ps", "z_done", "qk_done"))
        v_ps, v_done, sim_ps, sim_done, attn_done, gate_ps, gate_done = (
            sem(n) for n in ("v_ps", "v_done", "sim_ps", "sim_done", "attn_done", "gate_ps", "gate_done"))
        av_ps, gated_done, out_ps, base_done, t2_done = (
            sem(n) for n in ("av_ps", "gated_done", "out_ps", "base_done", "t2_done"))
        uvar_done, uscale_done, row_a_done, row_b_done, uT_ps, uT_done = (
            sem(n) for n in ("uvar_done", "uscale_done", "row_a_done", "row_b_done", "uT_ps", "uT_done"))
        logits_ps, in_row_done, prefix_ps, prefix_read, diff_done, tanh_done, slots_done = (
            sem(n) for n in ("logits_ps", "in_row_done", "prefix_ps", "prefix_read", "diff_done", "tanh_done",
                             "slots_done"))
        ids_done, scattered = sem("ids_done"), sem("scattered")
        ubias_done, u_rows_done = sem("ubias_done"), sem("u_rows_done")
        stored, padded = sem("stored"), sem("padded")
        tiles_done, pads_ready = sem("tiles_done"), sem("pads_ready")
        rows_in, sT_ps, sT_done, meta_done, h_ps, h_done, hT_ps, hT_done, y_ps, y_read, y_done, added = (
            sem(n) for n in ("rows_in", "sT_ps", "sT_done", "meta_done", "h_ps", "h_done", "hT_ps", "hT_done",
                             "y_ps", "y_read", "y_done", "added"))

        block = ctx.enter_context(nc.Block())

        CONV = dict(first=-3, last=IMAGES - 1, ahead=3, behind=0)
        ATTN = dict(first=-1, last=IMAGES, ahead=1, behind=1)
        MOE = dict(first=-1, last=MOE_TILES, ahead=1, behind=1)

        def absent(i, n=IMAGES):
            return isinstance(i, int) and not 0 <= i < n

        def tiles(i):
            return ds(i * HALVES, HALVES)

        def grouped(ap):
            return ap.rearrange("p t (g c) -> p t g c", c=GC)

        def over_row(ap):
            return ap.unsqueeze(2).broadcast_to((P, HALVES, D))

        def over_channels(ap):
            return ap.unsqueeze(1).unsqueeze(3).broadcast_to((P, HALVES, GROUPS, GC))

        @block.sync
        def _(sp):
            sp.dma_start(const[:, :], consts).then_inc(ld_const, 16)
            sp.dma_start(w1_sb[0:KC, :, :], w1).then_inc(ld_w1, 16)
            sp.dma_start(w1_sb[KC:KC + 1, NKC - 1, :], b1).then_inc(ld_w1, 16)
            xv = x.rearrange("(n p) c -> p n c", p=P)
            sp.dma_start(X[:, tiles(0), :], xv[:, tiles(0), :]).then_inc(ld_x, 16)
            with sp.Fori(1, IMAGES) as i:
                wait_alone(sp, ld_x, i * 16, ld_const)
                sp.dma_start(X[:, tiles(i), :], xv[:, tiles(i), :]).then_inc(ld_x, 16)

            sp.wait_ge(pads_ready, 1)
            sp.dma_start(out[TOKENS:TOKENS + P, :], pad_rows[:, 0:D]).then_inc(stored, 16)
            sp.dma_start(lists[SPARE:SPARE + P, :], pad_rows[:, :]).then_inc(padded, 16)

            ov = out[0:TOKENS, :].rearrange("(n p) c -> p n c", p=P)
            with sp.Fori(0, IMAGES) as i:
                wait_alone(sp, t2_done, i + 1, ld_const)
                sp.dma_start(ov[:, tiles(i), :], X[:, tiles(i), :]).then_inc(stored, 16)

            sp.wait_ge(tiles_done, 1)
            for e in range(EXPERTS):
                at = sp.value_load(list_end[0:1, e:e + 1], min_val=e * REGION, max_val=e * REGION + TOKENS)
                sp.dma_start(lists[ds(at, P), :], pad_rows[:, :]).then_inc(padded, 16)
            sp.wait_ge(padded, 16 * (EXPERTS + 1))
            sp.wait_ge(scattered, 16 * 2 * HALVES * IMAGES)

            def load_tile(j):
                at = sp.value_load(tile_row[0:1, ds(j, 1)], min_val=0, max_val=SPARE)
                sp.dma_start(slot_rows[:, :], lists[ds(at, P), :]).then_inc(rows_in, 16)

            load_tile(0)
            with sp.Fori(1, MOE_TILES) as j:
                wait_alone(sp, sT_ps, j, ld_const)
                sp.wait_ge(meta_done, j)
                load_tile(j)

        @block.gpsimd
        def _(pool):
            chain = Chain(pool, pool_self)
            for n, (dst, value) in enumerate(((coef[KC:KC + 1, NKC - 1, :], 1.0), (nT[KC:KC + 1, NKC - 1, :], 1.0),
                                              (sT[KC:KC + 1, NKC - 1, :], 1.0), (eps_sb[:, :], LN_EPS))):
                pool.memset(dst, value).then_inc(ones_set, 1)
                pool.wait_ge(ones_set, n + 1)
            chain.link(pool.memset(pad_rows[:, :], 0.0))
            pool.wait_ge(ld_const, 16)
            chain.link(pool.tensor_copy(pad_rows[:, D:D + 1].bitcast(i32), K("pad_id")))
            pool.tensor_copy(list_at[:, :], K("list_base")).then_inc(pads_ready, 1)
            for rows in (row_a, row_b):
                chain.link(pool.tensor_copy(rows[:, :, D:D + 1].bitcast(i32), K("ids").unsqueeze(2)))

            def conv_step(i):
                if not absent(i + 1):
                    wait(pool, gvar_done, i + 2)
                    chain.link(pool.tensor_tensor(grs[:, :], gvar[:, :], K("half"), ALU.pow))
                    wait(pool, coef_ps, i + 1)
                    pool.tensor_tensor(grouped(xn[:, :, :]), grouped(xc[:, :, :]), over_channels(grs[:, :]),
                                       ALU.mult).then_inc(xn_done, 1)

            pipeline(pool, conv_step, **CONV, chain=chain, per=1)

            def attn_step(i):
                r = i - 1
                if not absent(i):
                    whole = X[:, tiles(i), :]
                    wait_alone(pool, normed_done, i + 1, ld_const)
                    pool.tensor_tensor(whole, whole, over_row(r_scale[:, tiles(i)]), ALU.mult)
                    pool.drain()
                    pool.tensor_tensor(whole, whole, over_row(r_bias[:, tiles(i)]), ALU.add)
                    pool.drain()
                    pool.tensor_tensor(whole, whole, b_out_sb[:, :].unsqueeze(1).broadcast_to((P, HALVES, D)),
                                       ALU.add).then_inc(base_done, 1)
                if not absent(r):
                    wait_alone(pool, u_rows_done, r + 1, ld_const)
                    pool.tensor_copy(row_b[:, :, 0:D], row_a[:, :, 0:D]).then_inc(row_b_done, 1)
                    for rows in (row_a, row_b):
                        ids = rows[:, :, D:D + 1].bitcast(i32)
                        pool.tensor_scalar(ids, ids, SEQ, None, ALU.add).then_inc(ids_done, 1)
                    wait_alone(pool, ids_done, (r + 1) * 2, ld_const)
                    pool.wait_ge(row_a_done, r + 1)
                    pool.wait_ge(row_b_done, r + 1)
                    pool.wait_ge(slots_done, r + 1)
                    for c, rows in enumerate((row_a, row_b)):
                        for t in range(HALVES):
                            pool.indirect_dma_start(
                                out=lists, out_offset=bass.IndirectOffsetOnAxis(ap=slots[:, c, t:t + 1], axis=0),
                                in_=rows[:, t, :], in_offset=None).then_inc(scattered, 16)
                if not absent(i):
                    pool.wait_ge(uvar_done, i + 1)
                    pool.tensor_tensor(u_scale[:, :], u_var[:, :], K("half")[:, 0:HALVES],
                                       ALU.pow).then_inc(uscale_done, 1)
                if not absent(r):
                    pool.wait_ge(scattered, (r + 1) * (16 * 2 * HALVES))

            pool.wait_ge(ld_attn, 16 * 13)
            pool.wait_ge(scales_done, 1)
            pipeline(pool, attn_step, **ATTN)

            pool.wait_ge(stored, 16 * (IMAGES + 1))
            with pool.Fori(1, MOE_TILES + 1) as n:
                wait_alone(pool, y_done, n, ld_const)
                pool.indirect_dma_start(out=out, out_offset=bass.IndirectOffsetOnAxis(ap=y_id[:, 0:1], axis=0),
                                        in_=y_sb[:, :], in_offset=None, compute_op=ALU.add).then_inc(added, 16)
                pool.wait_ge(added, n * 16)

        @block.scalar
        def _(act):
            act.dma_start(w_hid_sb[0:KC, :, :], w_hid).then_inc(ld_attn, 16)
            act.dma_start(w_hid_sb[KC:KC + 1, NKC - 1, :], b_hid).then_inc(ld_attn, 16)
            act.dma_start(w_qk_sb[0:KC, :, :], w_qk).then_inc(ld_attn, 16)
            act.dma_start(w_qk_sb[KC:KC + 1, NKC - 1, :], b_qk).then_inc(ld_attn, 16)
            act.dma_start(w_out_sb[:, :, :], w_out).then_inc(ld_attn, 16)
            act.dma_start(ln_sb[:, 0, :], ln_w).then_inc(ld_attn, 16)
            act.dma_start(ln_sb[:, 1, :], ln_b).then_inc(ld_attn, 16)
            act.dma_start(gb_sb[:, 0:2], gamma).then_inc(ld_attn, 16)
            act.dma_start(gb_sb[:, 2:4], beta).then_inc(ld_attn, 16)
            act.dma_start(b_out_sb[:, :], b_out.partition_broadcast(P)).then_inc(ld_attn, 16)
            act.dma_start(w_r_sb[:, :, :], w_r).then_inc(ld_attn, 16)
            act.dma_start(b_o_sb[:, :, :], b_o.partition_broadcast(P)).then_inc(ld_attn, 16)
            act.dma_start(w_i_sb[KC:KC + 1, :, NKC - 1, :], b_i).then_inc(ld_attn, 16)
            act.dma_start(w_i_sb[0:KC, :, :, :], w_i).then_inc(ld_exp, 16)
            act.dma_start(w_o_sb[:, :, :, :], w_o).then_inc(ld_exp, 16)

            def conv_step(i):
                if not absent(i):
                    act.wait_ge(mix_ps, i + 1)
                    act.activation(mixed[:, :, :], ps_mix, ACT.Gelu).then_inc(mix_done, 1)
                if not absent(i + 2):
                    act.wait_ge(xc_done, i + 3)
                    act.activation(xsq[:, :, :], xc[:, :, :], ACT.Square).then_inc(sq_done, 1)
                if not absent(i + 1):
                    act.wait_ge(coef_ps, i + 2)
                    act.activation(coef[0:KC, :, :], ps_coef, ACT.Copy).then_inc(coef_done, 1)

            pipeline(act, conv_step, **CONV)

            act.wait_ge(ones_set, 4)
            act.wait_ge(mom_var, 1)
            act.activation(rs1[:, :], moments[:, :, 1], ACT.Sqrt, bias=eps_sb[:, :]).then_inc(mom_std, 1)
            act.wait_ge(mom2_var, 1)
            act.activation(n_bias[:, :], tmp32[:, :], ACT.Sqrt, bias=eps_sb[:, :]).then_inc(mom2_std, 1)
            act.wait_ge(ld_attn, 16 * 13)

            def attn_step(i):
                r = i - 1
                if not absent(i):
                    act.wait_ge(v_ps, i + 1)
                    act.activation(v_sb[:, :, :], ps_v, ACT.Silu).then_inc(v_done, 1)
                if not absent(i + 1):
                    wait(act, nT_ps, i + 1)
                    act.wait_ge(scales_done, 1)
                    for t in range(HALVES):
                        at = ds((i + 1) * HALVES + t, 1)
                        last = act.activation(normed[:, t, :].unsqueeze(1), X[:, at, :], ACT.Identity, bias=n_bias[:, at],
                                              scale=n_scale[:, at])
                    last.then_inc(normed_done, 1)
                if not absent(r):
                    act.wait_ge(uT_ps, r + 1)
                    act.activation(uT[:, :, :], ps_uT, ACT.Copy).then_inc(uT_done, 1)
                if not absent(i):
                    act.wait_ge(sim_ps, i + 1)
                    act.activation(simT[:, :, :], ps_sim, ACT.Relu, scale=1.0 / SEQ).then_inc(sim_done, 1)
                    act.wait_ge(gate_ps, i + 1)
                    act.activation(gateT[:, :, :], ps_gate, ACT.Silu).then_inc(gate_done, 1)
                if not absent(i + 1):
                    act.wait_ge(nT_ps, i + 2)
                    for k in range(NKC):
                        last = act.activation(nT[0:KC, k, :], ps_nT[:, k, :], ACT.Identity,
                                              bias=ln_sb[:, 1, k:k + 1], scale=ln_sb[:, 0, k:k + 1])
                    last.then_inc(nT_done, 1)
                    act.wait_ge(z_ps, i + 2)
                    act.activation(zT[:, :], ps_z, ACT.Silu).then_inc(z_done, 1)
                if not absent(r):
                    act.wait_ge(diff_done, r + 1)
                    act.activation(tanh_d[:, :], diff[:, :], ACT.Tanh, scale=0.5).then_inc(tanh_done, 1)

            pipeline(act, attn_step, **ATTN)

            with act.Fori(0, MOE_TILES) as j:
                act.wait_ge(h_ps, j + 1)
                act.activation(h_sb[:, :].rearrange("p (b n) -> p b n", b=2), ps_h, ACT.Gelu).then_inc(h_done, 1)

            act.wait_ge(added, 16 * MOE_TILES)
            act.wait_ge(stored, 16 * (IMAGES + 1))

        @block.vector
        def _(dve):
            chain = Chain(dve, dve_self)
            INV_GROUP = 1.0 / (SEQ * GC)

            def token_moments(i):
                for t in range(HALVES):
                    last = dve.bn_stats(stats[:, t, :], X[:, ds(i * HALVES + t, 1), :])
                dve.drain()
                for t in range(HALVES):
                    last = dve.bn_aggr(mom[:, t, :], stats[:, t, :])
                chain.link(last)

            def conv_step(i):
                if not absent(i + 1):
                    wait(dve, gsq_done, i + 2)
                    dve.tensor_scalar(gvar[:, :], ps_gsq, INV_GROUP, LN_EPS, ALU.mult,
                                      ALU.add).then_inc(gvar_done, 1)
                if not absent(i + 2):
                    wait(dve, gsum_done, i + 3)
                    chain.link(dve.tensor_scalar(gmean[:, :], ps_gsum, INV_GROUP, None, ALU.mult))
                    wait(dve, xn_done, i + 2)
                    dve.tensor_tensor(grouped(xc[:, :, :]), grouped(X[:, tiles(i + 2), :]),
                                      over_channels(gmean[:, :]), ALU.subtract).then_inc(xc_done, 1)
                if not absent(i + 3):
                    wait(dve, ld_x, (i + 4) * 16)
                    wait(dve, gsum_done, i + 3)
                    dve.tensor_reduce(gsum[:, :], grouped(X[:, tiles(i + 3), :]).rearrange("p t g c -> p g t c"),
                                      AX.XY, ALU.add).then_inc(gsum_in, 1)
                if not absent(i + 2):
                    wait(dve, sq_done, i + 3)
                    dve.tensor_reduce(gsq[:, :], grouped(xsq[:, :, :]).rearrange("p t g c -> p g t c"),
                                      AX.XY, ALU.add).then_inc(gsq_in, 1)
                if not absent(i):
                    wait(dve, conv_ps, i + 1)
                    ins = dve.tensor_tensor(X[:, tiles(i), :], X[:, tiles(i), :], ps_conv, ALU.add)
                    ins.then_inc(conv_read, 1)
                    wait_alone(dve, conv_read, i + 1, ld_const)
                    token_moments(i)
                    chain.link(dve.tensor_copy(moments[:, tiles(i), :], mom[:, :, :]))

            dve.wait_ge(ld_const, 16)
            pipeline(dve, conv_step, **CONV, chain=chain, per=3)

            mean, var = moments[:, :, 0], moments[:, :, 1]
            dve.engine_nop().then_inc(mom_var, 1)
            dve.wait_ge(mom_std, 1)
            chain.link(dve.reciprocal(rs1[:, :], rs1[:, :]))
            chain.link(dve.tensor_tensor(tmp32[:, :], var, rs1[:, :], ALU.mult))
            dve.tensor_tensor(tmp32[:, :], tmp32[:, :], rs1[:, :], ALU.mult).then_inc(mom2_var, 1)
            dve.tensor_scalar(r_scale[:, :], rs1[:, :], 1.0, None, ALU.add)
            dve.scalar_tensor_tensor(r_bias[:, :], mean, -1.0, rs1[:, :], ALU.mult, ALU.mult)
            dve.wait_ge(mom2_std, 1)
            chain.link(dve.reciprocal(n_scale[:, :], n_bias[:, :]))
            chain.link(dve.tensor_tensor(n_scale[:, :], n_scale[:, :], rs1[:, :], ALU.mult))
            dve.scalar_tensor_tensor(n_bias[:, :], mean, -1.0, n_scale[:, :], ALU.mult,
                                     ALU.mult).then_inc(scales_done, 1)

            def query_key(i):
                dve.wait_ge(z_done, i + 1)
                for n, dst in enumerate((qT, kT)):
                    last = dve.tensor_scalar(dst[:, :], zT[:, :], gb_sb[:, n:n + 1], gb_sb[:, 2 + n:3 + n],
                                             ALU.mult, ALU.add)
                last.then_inc(qk_done, 1)

            def choose(r):
                dve.wait_ge(logits_ps, r + 1)
                chain.link(dve.tensor_copy(logits[:, :, :], ps_logits))
                shape = (P, HALVES, EXPERTS, EXPERTS)
                other = logits[:, :, :].unsqueeze(2).broadcast_to(shape)
                own = logits[:, :, :].unsqueeze(3).broadcast_to(shape)
                dve.tensor_tensor(above[:, :, :, :], other, own, ALU.is_gt)
                chain.link(dve.tensor_tensor(equal[:, :, :, :], other, own, ALU.is_equal))
                lower = K("lower").rearrange("p (a b) -> p a b", b=EXPERTS).unsqueeze(1).broadcast_to(shape)
                chain.link(dve.tensor_tensor(equal[:, :, :, :], equal[:, :, :, :], lower, ALU.mult))
                chain.link(dve.tensor_tensor(above[:, :, :, :], above[:, :, :, :], equal[:, :, :, :], ALU.add))
                chain.link(dve.tensor_reduce(rank[:, :, :], above[:, :, :, :], AX.X, ALU.add))
                for c in range(2):
                    last = dve.tensor_scalar(chosen[:, c, :], rank[:, :, :].rearrange("p t e -> p (t e)"),
                                             float(c), None, ALU.is_equal)
                chain.link(last)
                by_expert = chosen[:, :, :].rearrange("p c (t e) -> p e c t", e=EXPERTS)
                dve.tensor_reduce(in_row[:, :], by_expert, AX.XY, ALU.add).then_inc(in_row_done, 1)
                dve.tensor_tensor(in_first[:, :], chosen[:, 0, 0:EXPERTS], chosen[:, 1, 0:EXPERTS], ALU.add)
                both = logits[:, :, :].rearrange("p t e -> p (t e)").unsqueeze(1).broadcast_to(
                    (P, 2, HALVES * EXPERTS))
                chain.link(dve.tensor_tensor(picked[:, :, :], chosen[:, :, :], both, ALU.mult))
                chain.link(dve.tensor_reduce(top[:, :, :], picked[:, :, :].rearrange(
                    "p c (t e) -> p c t e", e=EXPERTS), AX.X, ALU.add))
                dve.tensor_tensor(diff[:, :], top[:, 0, :], top[:, 1, :], ALU.subtract).then_inc(diff_done, 1)

            def place(r):
                dve.wait_ge(prefix_ps, r + 1)
                chain.link(dve.tensor_tensor(slot[:, 0, :], list_at[:, :], ps_rows_before, ALU.add))
                dve.tensor_tensor(slot[:, 1, :], slot[:, 0, :], in_first[:, :], ALU.add)
                ins = dve.tensor_tensor(list_at[:, :], list_at[:, :], ps_rows_all, ALU.add)
                ins.then_inc(prefix_read, 1)
                dve.wait_ge(prefix_read, r + 1)
                both = slot[:, :, :].rearrange("p t e -> p (t e)").unsqueeze(1).broadcast_to(
                    (P, 2, HALVES * EXPERTS))
                chain.link(dve.tensor_tensor(picked[:, :, :], chosen[:, :, :], both, ALU.mult))
                with nc.allow_low_precision(reason="whole numbers below 2**24"):
                    dve.tensor_reduce(slots[:, :, :], picked[:, :, :].rearrange("p c (t e) -> p c t e", e=EXPERTS),
                                      AX.X, ALU.add).then_inc(slots_done, 1)
                dve.wait_ge(tanh_done, r + 1)
                for rows, sign in ((row_a, 0.5), (row_b, -0.5)):
                    last = dve.tensor_scalar(rows[:, :, D + 1:D + 2], tanh_d[:, :].unsqueeze(2), sign, 0.5,
                                             ALU.mult, ALU.add)
                last.then_inc(row_a_done, 1)

            def attn_step(i):
                r = i - 1
                if not absent(i):
                    dve.wait_ge(sim_done, i + 1)
                    dve.tensor_tensor(attnT[:, :, :], simT[:, :, :], simT[:, :, :], ALU.mult).then_inc(attn_done, 1)
                if not absent(r):
                    choose(r)
                if not absent(i):
                    dve.wait_ge(gate_done, i + 1)
                    for k, (lo, hi) in enumerate(((0, 2), (2, 3))):
                        dve.wait_ge(av_ps, 2 * i + 1 + k)
                        dve.tensor_tensor(gatedT[:, lo:hi, :], ps_av[:, lo:hi, :], gateT[:, lo:hi, :],
                                          ALU.mult).then_inc(gated_done, 1)
                if not absent(i + 1):
                    query_key(i + 1)
                if not absent(r):
                    place(r)
                if not absent(i):
                    dve.wait_ge(out_ps, i + 1)
                    dve.wait_ge(base_done, i + 1)
                    ins = dve.tensor_tensor(X[:, tiles(i), :], X[:, tiles(i), :], ps_out, ALU.add)
                    ins.then_inc(t2_done, 1)
                    wait_alone(dve, t2_done, i + 1, ld_const)
                    token_moments(i)
                    dve.tensor_scalar(u_var[:, :], mom[:, :, 1], LN_EPS, None,
                                      ALU.add).then_inc(uvar_done, 1)
                    dve.wait_ge(uscale_done, i + 1)
                    ins = dve.scalar_tensor_tensor(u_bias[:, :], mom[:, :, 0], -1.0, u_scale[:, :],
                                                   ALU.mult, ALU.mult)
                    ins.then_inc(ubias_done, 1)
                    dve.wait_ge(ubias_done, i + 1)
                    wait(dve, scattered, i * (16 * 2 * HALVES))
                    for t in range(HALVES):
                        last = dve.tensor_scalar(row_a[:, t, 0:D], X[:, ds(i * HALVES + t, 1), :],
                                                 u_scale[:, t:t + 1], u_bias[:, t:t + 1], ALU.mult, ALU.add)
                    last.then_inc(u_rows_done, 1)

            dve.wait_ge(ld_attn, 16 * 13)
            dve.wait_ge(pads_ready, 1)
            pipeline(dve, attn_step, **ATTN, chain=chain, per=11)

            n_regions = (P, EXPERTS, TOKENS // P)
            n_all = (P, MOE_TILES, EXPERTS)
            dve.tensor_copy(list_end[:, :], list_at[:, :])
            chain.link(dve.tensor_tensor(n_list[:, :], list_at[:, :], K("list_base"), ALU.subtract))
            chain.link(dve.tensor_tensor(over[:, :, :], n_list[:, :].unsqueeze(2).broadcast_to(n_regions),
                                         K("tile_rows").unsqueeze(1).broadcast_to(n_regions), ALU.is_gt))
            chain.link(dve.tensor_reduce(n_tiles[:, :], over[:, :, :], AX.X, ALU.add))
            chain.link(dve.tensor_tensor_scan(t_end[:, :], K("ones")[:, 0:EXPERTS], n_tiles[:, :], 0.0,
                                              ALU.mult, ALU.add))
            chain.link(dve.tensor_tensor(t_start[:, :], t_end[:, :], n_tiles[:, :], ALU.subtract))
            tile_no = K("tile_no").unsqueeze(2).broadcast_to(n_all)

            def per_tile(ap):
                return ap.unsqueeze(1).broadcast_to(n_all)

            dve.scalar_tensor_tensor(base[:, :], t_start[:, :], -float(P), K("list_base"), ALU.mult, ALU.add)
            dve.tensor_tensor(started[:, :, :], tile_no, per_tile(t_start[:, :]), ALU.is_ge)
            chain.link(dve.tensor_tensor(ended[:, :, :], tile_no, per_tile(t_end[:, :]), ALU.is_ge))
            chain.link(dve.tensor_reduce(tile_f[:, :], ended[:, :, :], AX.X, ALU.add))
            dve.tensor_scalar(tile_expert[:, :], tile_f[:, :], float(EXPERTS - 1), None, ALU.min)
            dve.tensor_tensor(started[:, :, :], started[:, :, :], ended[:, :, :], ALU.subtract)
            chain.link(dve.scalar_tensor_tensor(rows_at[:, :, :], tile_no, float(P), per_tile(base[:, :]),
                                                ALU.mult, ALU.add))
            chain.link(dve.tensor_scalar(rows_at[:, :, :], rows_at[:, :, :], -float(SPARE), None, ALU.add))
            chain.link(dve.tensor_tensor(rows_at[:, :, :], rows_at[:, :, :], started[:, :, :], ALU.mult))
            chain.link(dve.tensor_reduce(tile_f[:, :], rows_at[:, :, :], AX.X, ALU.add))
            dve.tensor_scalar(tile_row[:, :], tile_f[:, :], float(SPARE), None,
                              ALU.add).then_inc(tiles_done, 1)
            dve.wait_ge(tiles_done, 1)

            def moe_step(j):
                if not absent(j, MOE_TILES):
                    for k in range(2):
                        dve.wait_ge(hT_ps, 2 * j + 1 + k)
                        dve.tensor_copy(hT[:, k * FF // 2:(k + 1) * FF // 2], ps_hT[:, k, :]).then_inc(hT_done, 1)
                if not absent(j + 1, MOE_TILES):
                    dve.wait_ge(sT_ps, j + 2)
                    dve.tensor_copy(sT[0:KC, :, :], ps_sT).then_inc(sT_done, 1)
                    dve.wait_ge(rows_in, (j + 2) * 16)
                    dve.tensor_copy(meta[:, ds(j + 1, 1), :], slot_rows[:, D:D + 2].bitcast(i32).unsqueeze(1)).then_inc(meta_done, 1)
                if not absent(j - 1, MOE_TILES):
                    p = j - 1
                    e = dve.value_load(tile_expert[0:1, ds(p, 1)], min_val=0, max_val=EXPERTS - 1)
                    dve.wait_ge(y_ps, p + 1)
                    wait(dve, added, p * 16)
                    ins = dve.tensor_tensor(y_sb[:, :].unsqueeze(1), ps_y.unsqueeze(1), b_o_sb[:, ds(e, 1), :], ALU.add)
                    ins.then_inc(y_read, 1)
                    dve.tensor_copy(y_id[:, :].unsqueeze(1), meta[:, ds(p, 1), 0:1])
                    dve.wait_ge(y_read, p + 1)
                    w = meta[:, ds(p, 1), 1:2].bitcast(f32)
                    dve.tensor_scalar(y_sb[:, :], y_sb[:, :], w.rearrange("p a b -> p (a b)"), None, ALU.mult).then_inc(y_done, 1)

            pipeline(dve, moe_step, **MOE)

        @block.tensor
        def _(pe):
            pe.wait_ge(ld_const, 16)
            pe.wait_ge(ld_w1, 32)
            pe.wait_ge(ones_set, 4)

            def mm(dst, lhsT, rhs, start=True, stop=True):
                return pe.matmul(dst, lhsT, rhs, start=start, stop=stop)

            def conv_step(i):
                if not absent(i + 1):
                    pe.wait_ge(gsq_in, i + 2)
                    mm(ps_gsq, K("ones"), gsq[:, :]).then_inc(gsq_done, 1)
                if not absent(i):
                    pe.wait_ge(coef_done, i + 1)
                    for f in range(NFC):
                        for k in range(NKC):
                            rows = KC + (k == NKC - 1)
                            last = mm(ps_mix[:, f, :], coef[0:rows, k, f * FCH:(f + 1) * FCH],
                                      w1_sb[0:rows, k, :], k == 0, k == NKC - 1)
                    last.then_inc(mix_ps, 1)
                if not absent(i + 1):
                    pe.wait_ge(xn_done, i + 2)
                    for k in range(NKC):
                        ch = slice(k * KC, (k + 1) * KC)
                        mm(ps_coef[:, k, 0:2 * FCH], xn[:, 0, ch], K("fwd0"), True, False)
                        mm(ps_coef[:, k, FCH:2 * FCH], xn[:, 1, ch], K("fwd1")[:, 0:FCH], False, True)
                        last = mm(ps_coef[:, k, 2 * FCH:3 * FCH], xn[:, 1, ch], K("fwd1")[:, FCH:2 * FCH])
                    last.then_inc(coef_ps, 1)
                if not absent(i + 3):
                    pe.wait_ge(gsum_in, i + 4)
                    wait(pe, xc_done, i + 3)
                    mm(ps_gsum, K("ones"), gsum[:, :]).then_inc(gsum_done, 1)
                if not absent(i):
                    pe.wait_ge(mix_done, i + 1)
                    wait(pe, conv_read, i)
                    mm(ps_conv[:, 0, :], K("inv0a", FCH), mixed[:, 0, :], True, False)
                    mm(ps_conv[:, 0, :], K("inv0b", FCH), mixed[:, 1, :], False, True)
                    mm(ps_conv[:, 1, :], K("inv1b", FCH), mixed[:, 1, :], True, False)
                    mm(ps_conv[:, 1, :], K("inv1c", FCH), mixed[:, 2, :], False, True).then_inc(conv_ps, 1)

            pipeline(pe, conv_step, **CONV)
            pe.wait_ge(ld_attn, 16 * 13)

            def z_product(i):
                pe.wait_ge(nT_done, i + 1)
                for k in range(NKC):
                    rows = KC + (k == NKC - 1)
                    last = mm(ps_z, w_qk_sb[0:rows, k, :], nT[0:rows, k, :], k == 0, k == NKC - 1)
                last.then_inc(z_ps, 1)

            def attn_step(i):
                r = i - 1
                if not absent(i):
                    for t in range(HALVES):
                        for k in range(NKC):
                            rows = KC + (k == NKC - 1)
                            last = mm(ps_v[:, t, :], nT[0:rows, k, t * P:(t + 1) * P], w_hid_sb[0:rows, k, 0:HID],
                                      k == 0, k == NKC - 1)
                    last.then_inc(v_ps, 1)
                if not absent(r):
                    pe.wait_ge(u_rows_done, r + 1)
                    wait(pe, prefix_read, r)
                    for t in range(HALVES):
                        for k in range(NKC):
                            last = pe.transpose(ps_uT[:, k, t * P:(t + 1) * P], row_a[:, t, k * KC:(k + 1) * KC],
                                                K("ident"))
                    last.then_inc(uT_ps, 1)
                if not absent(i):
                    pe.wait_ge(qk_done, i + 1)
                    for t in range(HALVES):
                        last = mm(ps_sim[:, t, :], kT[:, t * P:(t + 1) * P], qT[:, :])
                    last.then_inc(sim_ps, 1)
                    for c in range(HID // P):
                        for k in range(NKC):
                            rows = KC + (k == NKC - 1)
                            last = mm(ps_gate[:, c, :], w_hid_sb[0:rows, k, HID + c * P:HID + (c + 1) * P],
                                      nT[0:rows, k, :], k == 0, k == NKC - 1)
                    last.then_inc(gate_ps, 1)
                if not absent(r):
                    pe.wait_ge(uT_done, r + 1)
                    for t in range(HALVES):
                        for k in range(NKC):
                            last = mm(ps_logits[:, t, :], uT[:, k, t * P:(t + 1) * P], w_r_sb[:, k, :],
                                      k == 0, k == NKC - 1)
                    last.then_inc(logits_ps, 1)
                if not absent(i + 1):
                    pe.wait_ge(normed_done, i + 2)
                    for t in range(HALVES):
                        for k in range(NKC):
                            last = pe.transpose(ps_nT[:, k, t * P:(t + 1) * P], normed[:, t, k * KC:(k + 1) * KC],
                                                K("ident"))
                    last.then_inc(nT_ps, 1)
                if not absent(i):
                    pe.wait_ge(v_done, i + 1)
                    pe.wait_ge(attn_done, i + 1)
                    for c in range(HID // P):
                        for t in range(HALVES):
                            last = mm(ps_av[:, c, :], v_sb[:, t, c * P:(c + 1) * P], attnT[:, t, :],
                                      t == 0, t == HALVES - 1)
                        if c >= 1:
                            last.then_inc(av_ps, 1)
                if not absent(i + 1):
                    z_product(i + 1)
                if not absent(r):
                    pe.wait_ge(in_row_done, r + 1)
                    mm(ps_rows_before, K("before"), in_row[:, :])
                    mm(ps_rows_all, K("ones"), in_row[:, :]).then_inc(prefix_ps, 1)
                if not absent(i):
                    wait(pe, t2_done, i)
                    pe.wait_ge(gated_done, 2 * i + 2)
                    for t in range(HALVES):
                        for c in range(HID // P):
                            last = mm(ps_out[:, t, :], gatedT[:, c, t * P:(t + 1) * P], w_out_sb[:, c, :],
                                      c == 0, c == HID // P - 1)
                    last.then_inc(out_ps, 1)

            pipeline(pe, attn_step, **ATTN)

            pe.wait_ge(ld_exp, 32)
            pe.wait_ge(tiles_done, 1)

            def moe_step(j):
                if not absent(j, MOE_TILES):
                    e = pe.value_load(tile_expert[0:1, ds(j, 1)], min_val=0, max_val=EXPERTS - 1)
                    pe.wait_ge(sT_done, j + 1)
                    for b in range(2):
                        for k in range(NKC):
                            rows = KC + (k == NKC - 1)
                            last = mm(ps_h[:, b, :], sT[0:rows, k, :],
                                      w_i_sb[0:rows, ds(e, 1), k, b * FF // 2:(b + 1) * FF // 2],
                                      k == 0, k == NKC - 1)
                    last.then_inc(h_ps, 1)
                if not absent(j - 1, MOE_TILES):
                    p = j - 1
                    e = pe.value_load(tile_expert[0:1, ds(p, 1)], min_val=0, max_val=EXPERTS - 1)
                    pe.wait_ge(hT_done, 2 * p + 2)
                    wait(pe, y_read, p)
                    for f in range(FCHUNKS):
                        last = mm(ps_y, hT[:, f * P:(f + 1) * P], w_o_sb[:, ds(e, 1), f, :], f == 0,
                                  f == FCHUNKS - 1)
                    last.then_inc(y_ps, 1)
                if not absent(j, MOE_TILES):
                    pe.wait_ge(h_done, j + 1)
                    for f in range(FCHUNKS):
                        b, c = divmod(f, FCHUNKS // 2)
                        last = pe.transpose(ps_hT[:, b, c * P:(c + 1) * P], h_sb[:, f * P:(f + 1) * P], K("ident"))
                        if c == FCHUNKS // 2 - 1:
                            last.then_inc(hT_ps, 1)
                if not absent(j + 1, MOE_TILES):
                    pe.wait_ge(rows_in, (j + 2) * 16)
                    for k in range(NKC):
                        last = pe.transpose(ps_sT[:, k, :], slot_rows[:, k * KC:(k + 1) * KC], K("ident"))
                    last.then_inc(sT_ps, 1)

            pipeline(pe, moe_step, **MOE)


def kernel(x, L0_conv_W1, L0_conv_b1, L1_attn_ln_w, L1_attn_ln_b, L1_attn_W_hidden, L1_attn_b_hidden,
           L1_attn_W_qk, L1_attn_b_qk, L1_attn_gamma, L1_attn_beta, L1_attn_W_out, L1_attn_b_out,
           L1_ffn_Wr, L1_ffn_Wi, L1_ffn_bi, L1_ffn_Wo, L1_ffn_bo):
    import concourse.bacc as bacc
    from concourse.bass_utils import run_bass_kernel_spmd

    def packed(w, rows):
        w = np.asarray(w)
        w = w.reshape(*w.shape[:-1], w.shape[-1] // rows, rows)
        w = np.swapaxes(w, -3, -2)
        return np.ascontiguousarray(np.moveaxis(w, -1, 0))

    def columns(v):
        return np.ascontiguousarray(np.asarray(v).reshape(NKC, KC).T)

    arrays = {
        "x": np.asarray(x).reshape(TOKENS, D), "consts": shape_constants(),
        "w1": packed(L0_conv_W1, KC), "b1": np.asarray(L0_conv_b1).reshape(1, D),
        "ln_w": columns(L1_attn_ln_w), "ln_b": columns(L1_attn_ln_b),
        "w_hid": packed(L1_attn_W_hidden, KC), "b_hid": np.asarray(L1_attn_b_hidden).reshape(1, 2 * HID),
        "w_qk": packed(L1_attn_W_qk, KC), "b_qk": np.asarray(L1_attn_b_qk).reshape(1, QK),
        "gamma": np.ascontiguousarray(np.asarray(L1_attn_gamma).T),
        "beta": np.ascontiguousarray(np.asarray(L1_attn_beta).T),
        "w_out": packed(L1_attn_W_out, P), "b_out": np.asarray(L1_attn_b_out),
        "w_r": packed(L1_ffn_Wr, KC),
        "w_i": packed(L1_ffn_Wi, KC), "b_i": np.asarray(L1_ffn_bi).reshape(1, EXPERTS, FF),
        "w_o": packed(L1_ffn_Wo, P), "b_o": np.asarray(L1_ffn_bo),
    }
    nc = bacc.Bacc("TRN2", target_bir_lowering=False, num_devices=1)
    aps = [nc.dram_tensor(f"in_{n}", a.shape, mybir.dt.from_np(a.dtype), kind="ExternalInput").ap()
           for n, a in arrays.items()]
    out = nc.dram_tensor("out_rows", (TOKENS + P, D), mybir.dt.float32, kind="ExternalOutput").ap()
    names = dict(zip(arrays, aps))
    build(nc, **names, out=out)
    r = run_bass_kernel_spmd(nc, [{f"in_{n}": a for n, a in arrays.items()}], core_ids=[0])
    return r.results[0]["out_rows"][:TOKENS].reshape(IMAGES, SIDE, SIDE, D)
```

```python
from contextlib import ExitStack

import numpy as np
import concourse.bass as bass
from concourse import mybir

IMAGES, SIDE, D = 16, 16, 192
TOKENS = IMAGES * SIDE * SIDE
SEQ = SIDE * SIDE
P = 128
HALVES = SEQ // P
GROUPS = 32
GC = D // GROUPS
BLOCK = 3
BROWS = -(-SIDE // BLOCK)
FCH = 2 * BROWS * BLOCK * BLOCK
NFC = BROWS // 2
KC = 96
NKC = D // KC
HID = 2 * D
QK = 32
EXPERTS, FF = 8, 768
FCHUNKS = FF // P
REGION = TOKENS + P
SPARE = EXPERTS * REGION
ROW = D + 2
MOE_TILES = (2 * TOKENS + EXPERTS * (P - 1)) // P
LN_EPS = 1e-5

_WIDTHS = [("ident", P), ("ones", P), ("before", P), ("fwd0", 2 * FCH), ("fwd1", 2 * FCH),
           ("inv0a", P), ("inv0b", P), ("inv1b", P), ("inv1c", P), ("lower", EXPERTS * EXPERTS),
           ("list_base", EXPERTS), ("tile_rows", TOKENS // P), ("tile_no", MOE_TILES), ("ids", HALVES),
           ("pad_id", 1)]
CONST_AT, CONST_W = {}, 0
for _n, _w in _WIDTHS:
    CONST_AT[_n] = (CONST_W, CONST_W + _w)
    CONST_W += _w


def shape_constants():
    c = np.zeros((P, CONST_W), np.float32)

    def put(name, a):
        lo, _ = CONST_AT[name]
        c[:a.shape[0], lo:lo + a.shape[1]] = a

    k, n = np.arange(BLOCK)[:, None], np.arange(BLOCK)[None, :]
    dct = np.cos(np.pi / BLOCK * (n + 0.5) * k) * np.where(k == 0, np.sqrt(1 / BLOCK), np.sqrt(2 / BLOCK))
    fwd = np.zeros((SEQ, NFC * FCH))
    inv = np.zeros((NFC * FCH, SEQ))
    for bh in range(BROWS):
        for bw in range(BROWS):
            for a in range(BLOCK):
                for b in range(BLOCK):
                    f = ((bh * BROWS + bw) * BLOCK + a) * BLOCK + b
                    for r in range(BLOCK):
                        for s in range(BLOCK):
                            h, w = bh * BLOCK + r, bw * BLOCK + s
                            fwd[min(h, SIDE - 1) * SIDE + min(w, SIDE - 1), f] += dct[a, r] * dct[b, s]
                            if h < SIDE and w < SIDE:
                                inv[f, h * SIDE + w] = dct[a, r] * dct[b, s]
    assert not fwd[:P, 2 * FCH:].any() and not fwd[P:, :FCH].any()
    put("ident", np.eye(P))
    put("ones", np.ones((P, P)))
    put("before", np.triu(np.ones((P, P)), 1))
    put("fwd0", fwd[:P, :2 * FCH])
    put("fwd1", fwd[P:, FCH:])
    put("inv0a", inv[:FCH, :P])
    put("inv0b", inv[FCH:2 * FCH, :P])
    put("inv1b", inv[FCH:2 * FCH, P:])
    put("inv1c", inv[2 * FCH:, P:])
    assert not inv[:FCH, P:].any() and not inv[2 * FCH:, :P].any()
    every = np.ones((P, 1))
    put("lower", every * np.tril(np.ones((EXPERTS, EXPERTS)), -1).reshape(1, -1))
    put("list_base", every * (np.arange(EXPERTS) * REGION)[None])
    put("tile_rows", every * (np.arange(TOKENS // P) * P)[None])
    put("tile_no", every * np.arange(MOE_TILES)[None])
    put("ids", np.arange(P)[:, None] + P * np.arange(HALVES)[None] - SEQ)
    put("pad_id", TOKENS + np.arange(P)[:, None])
    return c


def wait(eng, sem, value):
    if isinstance(value, int) and value <= 0:
        return
    eng.wait_ge(sem, value)


def wait_alone(eng, sem, value, held):
    eng.wait_ge(held, 16)
    eng.wait_ge(sem, value)


class Chain:

    def __init__(self, eng, sem):
        self.eng, self.sem, self.count, self.extra = eng, sem, 0, 0

    def mark(self, ins):
        ins.then_inc(self.sem, 1)
        self.count += 1

    def wait(self):
        self.eng.wait_ge(self.sem, self.count + self.extra)

    def link(self, ins):
        self.mark(ins)
        self.wait()


def pipeline(eng, step, first, last, ahead, behind, chain=None, per=0):
    n = last + 1 - behind
    lo, hi = behind + 1, n - ahead
    for i in range(first, lo):
        step(i)
    with eng.Fori(lo, hi) as i:
        if chain:
            start = chain.count
            chain.extra = (i - lo) * per
        step(i)
    if chain:
        assert chain.count - start == per, (chain.count - start, per)
        chain.count = start + per * (hi - lo)
        chain.extra = 0
    for i in range(hi, last + 1):
        step(i)


def build(nc, x, consts, w1, b1, ln_w, ln_b, w_hid, b_hid, w_qk, b_qk, gamma, beta, w_out, b_out,
          w_r, w_i, b_i, w_o, b_o, out):
    f32, i32 = mybir.dt.float32, mybir.dt.int32
    ALU, ACT, AX = mybir.AluOpType, mybir.ActivationFunctionType, mybir.AxisListType
    ds = bass.ds

    lists = nc.dram_tensor("lists", (SPARE + P, ROW), f32, kind="Internal").ap()

    ctx = ExitStack()
    with ctx:
        def sb(name, shape, dt=f32):
            return ctx.enter_context(nc.sbuf_tensor(name, shape, dt))

        def sem(name):
            return ctx.enter_context(nc.semaphore(name))

        const = sb("const", [P, CONST_W])

        def K(name, rows=P):
            lo, hi = CONST_AT[name]
            return const[0:rows, lo:hi]

        X = sb("X", [P, IMAGES * HALVES, D])
        moments = sb("moments", [P, IMAGES * HALVES, 2])

        w1_sb = sb("w1_sb", [KC + 1, NKC, D])
        gsum = sb("gsum", [P, GROUPS])
        gsq = sb("gsq", [P, GROUPS])
        gmean = sb("gmean", [P, GROUPS])
        gvar = sb("gvar", [P, GROUPS])
        grs = sb("grs", [P, GROUPS])
        gneg = sb("gneg", [P, GROUPS])
        newton = sb("newton", [P, GROUPS])
        xsq = sb("xsq", [P, HALVES, D])
        xn = sb("xn", [P, HALVES, D])
        coef = sb("coef", [KC + 1, NKC, NFC * FCH])
        mixed = sb("mixed", [FCH, NFC, D])
        stats = sb("stats", [P, HALVES, 6])
        mom = sb("mom", [P, HALVES, 2])

        w_hid_sb = sb("w_hid_sb", [KC + 1, NKC, 2 * HID])
        w_qk_sb = sb("w_qk_sb", [KC + 1, NKC, QK])
        w_out_sb = sb("w_out_sb", [P, HID // P, D])
        ln_sb = sb("ln_sb", [KC, 2, NKC])
        gb_sb = sb("gb_sb", [QK, 4])
        b_out_sb = sb("b_out_sb", [P, D])
        w_r_sb = sb("w_r_sb", [KC, NKC, EXPERTS])
        rs1 = sb("rs1", [P, IMAGES * HALVES])
        tmp32 = sb("tmp32", [P, IMAGES * HALVES])
        n_scale = sb("n_scale", [P, IMAGES * HALVES])
        n_bias = sb("n_bias", [P, IMAGES * HALVES])
        r_scale = sb("r_scale", [P, IMAGES * HALVES])
        r_bias = sb("r_bias", [P, IMAGES * HALVES])
        eps_sb = sb("eps_sb", [P, 1])
        normed = sb("normed", [P, HALVES, D])
        nT = sb("nT", [KC + 1, NKC, SEQ])
        zT = sb("zT", [QK, SEQ])
        qT = sb("qT", [QK, SEQ])
        kT = sb("kT", [QK, SEQ])
        v_sb = sb("v_sb", [P, HALVES, HID])
        gateT = sb("gateT", [P, HID // P, SEQ])
        simT = sb("simT", [P, HALVES, SEQ])
        attnT = sb("attnT", [P, HALVES, SEQ])
        gatedT = sb("gatedT", [P, HID // P, SEQ])

        u_var = sb("u_var", [P, HALVES])
        u_neg = sb("u_neg", [P, HALVES])
        u_scale = sb("u_scale", [P, HALVES])
        u_bias = sb("u_bias", [P, HALVES])
        row_a = sb("row_a", [P, HALVES, ROW])
        row_b = sb("row_b", [P, HALVES, ROW])
        uT = sb("uT", [KC, NKC, SEQ])
        logits = sb("logits", [P, HALVES, EXPERTS])
        above = sb("above", [P, HALVES, EXPERTS, EXPERTS])
        equal = sb("equal", [P, HALVES, EXPERTS, EXPERTS])
        rank = sb("rank", [P, HALVES, EXPERTS])
        chosen = sb("chosen", [P, 2, HALVES * EXPERTS])
        in_row = sb("in_row", [P, EXPERTS])
        in_first = sb("in_first", [P, EXPERTS])
        picked = sb("picked", [P, 2, HALVES * EXPERTS])
        top = sb("top", [P, 2, HALVES])
        diff = sb("diff", [P, HALVES])
        tanh_d = sb("tanh_d", [P, HALVES])
        list_at = sb("list_at", [P, EXPERTS])
        slot = sb("slot", [P, HALVES, EXPERTS])
        slots = sb("slots", [P, 2, HALVES], i32)
        pad_rows = sb("pad_rows", [P, ROW])

        n_list = sb("n_list", [P, EXPERTS])
        over = sb("over", [P, EXPERTS, TOKENS // P])
        n_tiles = sb("n_tiles", [P, EXPERTS])
        t_end = sb("t_end", [P, EXPERTS])
        t_start = sb("t_start", [P, EXPERTS])
        base = sb("base", [P, EXPERTS])
        started = sb("started", [P, MOE_TILES, EXPERTS])
        ended = sb("ended", [P, MOE_TILES, EXPERTS])
        rows_at = sb("rows_at", [P, MOE_TILES, EXPERTS])
        tile_f = sb("tile_f", [P, MOE_TILES])
        tile_expert = sb("tile_expert", [P, MOE_TILES], i32)
        tile_row = sb("tile_row", [P, MOE_TILES], i32)
        list_end = sb("list_end", [P, EXPERTS], i32)

        w_i_sb = sb("w_i_sb", [KC + 1, EXPERTS, NKC, FF])
        w_o_sb = sb("w_o_sb", [P, EXPERTS, FCHUNKS, D])
        xc = w_o_sb[:, :, :, :].rearrange("p e f c -> p (e f) c")[:, 0:IMAGES * HALVES, :]
        b_o_sb = sb("b_o_sb", [P, EXPERTS, D])
        slot_rows = sb("slot_rows", [P, ROW])
        meta = sb("meta", [P, MOE_TILES, 2], i32)
        sT = sb("sT", [KC + 1, NKC, P])
        h_sb = sb("h_sb", [P, FF])
        hT = sb("hT", [P, FF])
        y_sb = sb("y_sb", [P, D])
        y_id = sb("y_id", [P, 1], i32)

        ps = ctx.enter_context(nc.psum_tensor("ps", [P, 8, 512], f32))

        ps_coef = ps[0:KC, 0:2, 0:NFC * FCH]
        ps_mix = ps[:, 2:4, :].rearrange("p b (k c) -> p (b k) c", c=256)[0:FCH, 0:NFC, 0:D]
        ps_conv = ps[:, 4, 0:HALVES * D].rearrange("p (t c) -> p t c", c=D)
        ps_gsum, ps_gsq = ps[:, 5, 0:GROUPS], ps[:, 6, 0:GROUPS]
        ps_nT = ps[0:KC, 0, :].rearrange("p (k n) -> p k n", k=NKC)
        ps_z = ps[0:QK, 1, 0:SEQ]
        ps_sim = ps[:, 1, :].rearrange("p (t n) -> p t n", t=HALVES)
        ps_v = ps[:, 2:4, 0:HID]
        ps_av = ps[:, 2:4, :].rearrange("p b (k n) -> p (b k) n", n=SEQ)[:, 0:HID // P, :]
        ps_gate = ps[:, 4:6, :].rearrange("p b (k n) -> p (b k) n", n=SEQ)[:, 0:HID // P, :]
        ps_out = ps[:, 6, 0:HALVES * D].rearrange("p (t c) -> p t c", c=D)
        ps_uT = ps[0:KC, 7, :].rearrange("p (k n) -> p k n", k=NKC)
        ps_logits = ps[:, 7, 0:HALVES * EXPERTS].rearrange("p (t e) -> p t e", e=EXPERTS)
        ps_rows_before = ps[:, 7, 64:64 + EXPERTS]
        ps_rows_all = ps[:, 7, 128:128 + EXPERTS]
        ps_h = ps[:, 0:2, 0:FF // 2]
        ps_hT = ps[:, 2:4, 0:FF // 2]
        ps_sT = ps[0:KC, 4, 0:NKC * P].rearrange("p (k n) -> p k n", k=NKC)
        ps_y = ps[:, 5, 0:D]

        ld_const, ld_w1, ld_x, ld_attn, ld_exp = (sem(f"ld_{n}") for n in ("const", "w1", "x", "attn", "exp"))
        ones_set = sem("ones_set")
        dve_self, act_self, pool_self = sem("dve_self"), sem("act_self"), sem("pool_self")
        gsum_in, gsum_done = sem("gsum_in"), sem("gsum_done")
        xc_done, sq_done = sem("xc_done"), sem("sq_done")
        gsq_in, gsq_done, grs_done, xn_done = sem("gsq_in"), sem("gsq_done"), sem("grs_done"), sem("xn_done")
        gmean_done = sem("gmean_done")
        coef_ps, coef_done = sem("coef_ps"), sem("coef_done")
        mix_ps, mix_done, conv_ps, conv_read, conv_done = (
            sem(n) for n in ("mix_ps", "mix_done", "conv_ps", "conv_read", "conv_done"))
        mom_var, mom_std, mom2_var, mom2_std, scales_done = (
            sem(n) for n in ("mom_var", "mom_std", "mom2_var", "mom2_std", "scales_done"))
        normed_done, nT_ps, nT_done, z_ps, z_done, qk_done = (
            sem(n) for n in ("normed_done", "nT_ps", "nT_done", "z_ps", "z_done", "qk_done"))
        v_ps, v_done, sim_ps, sim_done, attn_done, gate_ps, gate_done = (
            sem(n) for n in ("v_ps", "v_done", "sim_ps", "sim_done", "attn_done", "gate_ps", "gate_done"))
        av_ps, gated_done, out_ps, base_done, t2_done = (
            sem(n) for n in ("av_ps", "gated_done", "out_ps", "base_done", "t2_done"))
        row_a_done, row_b_done, uT_ps, uT_done = (
            sem(n) for n in ("row_a_done", "row_b_done", "uT_ps", "uT_done"))
        logits_ps, in_row_done, prefix_ps, prefix_read, diff_done, tanh_done, slots_done = (
            sem(n) for n in ("logits_ps", "in_row_done", "prefix_ps", "prefix_read", "diff_done", "tanh_done",
                             "slots_done"))
        ids_done, scattered = sem("ids_done"), sem("scattered")
        u_rows_done, sum_done = sem("u_rows_done"), sem("sum_done")
        stored, padded = sem("stored"), sem("padded")
        tiles_done, pads_ready = sem("tiles_done"), sem("pads_ready")
        rows_in, sT_ps, sT_done, meta_done, h_ps, h_done, hT_ps, hT_done, y_ps, y_read, y_done, added = (
            sem(n) for n in ("rows_in", "sT_ps", "sT_done", "meta_done", "h_ps", "h_done", "hT_ps", "hT_done",
                             "y_ps", "y_read", "y_done", "added"))

        block = ctx.enter_context(nc.Block())

        CONV = dict(first=-4, last=IMAGES, ahead=4, behind=1)
        ATTN = dict(first=-1, last=IMAGES, ahead=1, behind=1)
        MOE = dict(first=-1, last=MOE_TILES, ahead=1, behind=1)

        def absent(i, n=IMAGES):
            return isinstance(i, int) and not 0 <= i < n

        def tiles(i):
            return ds(i * HALVES, HALVES)

        def grouped(ap):
            return ap.rearrange("p t (g c) -> p t g c", c=GC)

        def over_channels(ap):
            return ap.unsqueeze(1).unsqueeze(3).broadcast_to((P, HALVES, GROUPS, GC))

        @block.sync
        def _(sp):
            xv = x.rearrange("(n p) c -> p n c", p=P)
            sp.dma_start(X[:, tiles(0), :], xv[:, tiles(0), :]).then_inc(ld_x, 16)
            sp.dma_start(const[:, :], consts).then_inc(ld_const, 16)
            with sp.Fori(1, IMAGES) as i:
                wait_alone(sp, ld_x, i * 16, ld_const)
                sp.dma_start(X[:, tiles(i), :], xv[:, tiles(i), :]).then_inc(ld_x, 16)

            sp.wait_ge(pads_ready, 1)
            sp.dma_start(out[TOKENS:TOKENS + P, :], pad_rows[:, 0:D]).then_inc(stored, 16)
            sp.dma_start(lists[SPARE:SPARE + P, :], pad_rows[:, :]).then_inc(padded, 16)

            ov = out[0:TOKENS, :].rearrange("(n p) c -> p n c", p=P)
            with sp.Fori(0, IMAGES) as i:
                wait_alone(sp, t2_done, i + 1, ld_const)
                sp.dma_start(ov[:, tiles(i), :], X[:, tiles(i), :]).then_inc(stored, 16)

            sp.wait_ge(tiles_done, 1)
            for e in range(EXPERTS):
                at = sp.value_load(list_end[0:1, e:e + 1], min_val=e * REGION, max_val=e * REGION + TOKENS)
                sp.dma_start(lists[ds(at, P), :], pad_rows[:, :]).then_inc(padded, 16)
            sp.wait_ge(padded, 16 * (EXPERTS + 1))
            sp.wait_ge(scattered, 16 * 2 * HALVES * IMAGES)

            def load_tile(j):
                at = sp.value_load(tile_row[0:1, ds(j, 1)], min_val=0, max_val=SPARE)
                sp.dma_start(slot_rows[:, :], lists[ds(at, P), :]).then_inc(rows_in, 16)

            load_tile(0)
            with sp.Fori(1, MOE_TILES) as j:
                wait_alone(sp, sT_ps, j, ld_const)
                sp.wait_ge(meta_done, j)
                load_tile(j)

        @block.gpsimd
        def _(pool):
            chain = Chain(pool, pool_self)
            for n, (dst, value) in enumerate(((coef[KC:KC + 1, NKC - 1, :], 1.0), (nT[KC:KC + 1, NKC - 1, :], 1.0),
                                              (sT[KC:KC + 1, NKC - 1, :], 1.0), (eps_sb[:, :], LN_EPS))):
                pool.memset(dst, value).then_inc(ones_set, 1)
                pool.wait_ge(ones_set, n + 1)
            chain.link(pool.memset(pad_rows[:, :], 0.0))
            pool.wait_ge(ld_const, 16)
            chain.link(pool.tensor_copy(pad_rows[:, D:D + 1].bitcast(i32), K("pad_id")))
            pool.tensor_copy(list_at[:, :], K("list_base")).then_inc(pads_ready, 1)
            for rows in (row_a, row_b):
                chain.link(pool.tensor_copy(rows[:, :, D:D + 1].bitcast(i32), K("ids").unsqueeze(2)))

            def conv_step(i):
                if not absent(i + 3):
                    wait_alone(pool, gmean_done, i + 4, ld_const)
                    pool.tensor_tensor(grouped(xc[:, tiles(i + 3), :]), grouped(X[:, tiles(i + 3), :]),
                                       over_channels(gmean[:, :]), ALU.subtract).then_inc(xc_done, 1)
                if not absent(i + 2):
                    wait_alone(pool, grs_done, i + 3, ld_const)
                    wait(pool, coef_ps, i + 2)
                    pool.tensor_tensor(grouped(xn[:, :, :]), grouped(xc[:, tiles(i + 2), :]),
                                       over_channels(grs[:, :]), ALU.mult).then_inc(xn_done, 1)

            pipeline(pool, conv_step, **CONV)

            def attn_step(i):
                r = i - 1
                if not absent(i):
                    whole = X[:, tiles(i), :]
                    wait_alone(pool, sum_done, i + 1, ld_const)
                    pool.tensor_tensor(whole, whole, b_out_sb[:, :].unsqueeze(1).broadcast_to((P, HALVES, D)),
                                       ALU.add).then_inc(base_done, 1)
                if not absent(r):
                    for rows in (row_a, row_b):
                        ids = rows[:, :, D:D + 1].bitcast(i32)
                        pool.tensor_scalar(ids, ids, SEQ, None, ALU.add).then_inc(ids_done, 1)
                    wait_alone(pool, ids_done, (r + 1) * 2, ld_const)
                    pool.wait_ge(row_a_done, r + 1)
                    pool.wait_ge(row_b_done, r + 1)
                    pool.wait_ge(slots_done, r + 1)
                    for c, rows in enumerate((row_a, row_b)):
                        for t in range(HALVES):
                            pool.indirect_dma_start(
                                out=lists, out_offset=bass.IndirectOffsetOnAxis(ap=slots[:, c, t:t + 1], axis=0),
                                in_=rows[:, t, :], in_offset=None).then_inc(scattered, 16)
                if not absent(r):
                    pool.wait_ge(scattered, (r + 1) * (16 * 2 * HALVES))

            pool.wait_ge(ld_attn, 16 * 13)
            pool.wait_ge(scales_done, 1)
            pipeline(pool, attn_step, **ATTN)

            pool.wait_ge(stored, 16 * (IMAGES + 1))
            with pool.Fori(1, MOE_TILES + 1) as n:
                wait_alone(pool, y_done, n, ld_const)
                pool.indirect_dma_start(out=out, out_offset=bass.IndirectOffsetOnAxis(ap=y_id[:, 0:1], axis=0),
                                        in_=y_sb[:, :], in_offset=None, compute_op=ALU.add).then_inc(added, 16)
                pool.wait_ge(added, n * 16)

        @block.scalar
        def _(act):
            act.dma_start(w1_sb[0:KC, :, :], w1).then_inc(ld_w1, 16)
            act.dma_start(w1_sb[KC:KC + 1, NKC - 1, :], b1).then_inc(ld_w1, 16)
            act.wait_ge(ld_x, 16 * 4)
            act.dma_start(w_hid_sb[0:KC, :, :], w_hid).then_inc(ld_attn, 16)
            act.dma_start(w_hid_sb[KC:KC + 1, NKC - 1, :], b_hid).then_inc(ld_attn, 16)
            act.dma_start(w_qk_sb[0:KC, :, :], w_qk).then_inc(ld_attn, 16)
            act.dma_start(w_qk_sb[KC:KC + 1, NKC - 1, :], b_qk).then_inc(ld_attn, 16)
            act.dma_start(w_out_sb[:, :, :], w_out).then_inc(ld_attn, 16)
            act.dma_start(ln_sb[:, 0, :], ln_w).then_inc(ld_attn, 16)
            act.dma_start(ln_sb[:, 1, :], ln_b).then_inc(ld_attn, 16)
            act.dma_start(gb_sb[:, 0:2], gamma).then_inc(ld_attn, 16)
            act.dma_start(gb_sb[:, 2:4], beta).then_inc(ld_attn, 16)
            act.dma_start(b_out_sb[:, :], b_out.partition_broadcast(P)).then_inc(ld_attn, 16)
            act.dma_start(w_r_sb[:, :, :], w_r).then_inc(ld_attn, 16)
            act.dma_start(b_o_sb[:, :, :], b_o.partition_broadcast(P)).then_inc(ld_attn, 16)
            act.dma_start(w_i_sb[KC:KC + 1, :, NKC - 1, :], b_i).then_inc(ld_attn, 16)

            def conv_step(i):
                if not absent(i + 3):
                    act.wait_ge(xc_done, i + 4)
                    wait(act, gsq_in, i + 3)
                    act.activation(xsq[:, :, :], xc[:, tiles(i + 3), :], ACT.Square).then_inc(sq_done, 1)
                if not absent(i):
                    act.wait_ge(mix_ps, i + 1)
                    act.activation(mixed[:, :, :], ps_mix, ACT.Gelu).then_inc(mix_done, 1)
                if not absent(i + 1):
                    act.wait_ge(coef_ps, i + 2)
                    act.activation(coef[0:KC, :, :], ps_coef, ACT.Copy).then_inc(coef_done, 1)

            pipeline(act, conv_step, **CONV)

            act.dma_start(w_i_sb[0:KC, :, :, :], w_i).then_inc(ld_exp, 16)
            act.wait_ge(xn_done, IMAGES)
            act.dma_start(w_o_sb[:, :, :, :], w_o).then_inc(ld_exp, 16)

            act.wait_ge(ones_set, 4)
            act.wait_ge(mom_var, 1)
            act.activation(rs1[:, :], moments[:, :, 1], ACT.Sqrt, bias=eps_sb[:, :]).then_inc(mom_std, 1)
            act.wait_ge(mom2_var, 1)
            act.activation(n_bias[:, :], tmp32[:, :], ACT.Sqrt, bias=eps_sb[:, :]).then_inc(mom2_std, 1)
            act.wait_ge(ld_attn, 16 * 13)

            def attn_step(i):
                r = i - 1
                if not absent(i):
                    act.wait_ge(v_ps, i + 1)
                    act.activation(v_sb[:, :, :], ps_v, ACT.Silu).then_inc(v_done, 1)
                if not absent(i + 1):
                    wait(act, nT_ps, i + 1)
                    act.wait_ge(scales_done, 1)
                    for t in range(HALVES):
                        at = ds((i + 1) * HALVES + t, 1)
                        last = act.activation(normed[:, t, :].unsqueeze(1), X[:, at, :], ACT.Identity, bias=n_bias[:, at],
                                              scale=n_scale[:, at])
                    last.then_inc(normed_done, 1)
                if not absent(i):
                    act.wait_ge(normed_done, i + 1)
                    for t in range(HALVES):
                        at = ds(i * HALVES + t, 1)
                        last = act.activation(X[:, at, :], X[:, at, :], ACT.Identity, bias=r_bias[:, at],
                                              scale=r_scale[:, at])
                    last.then_inc(sum_done, 1)
                if not absent(i):
                    act.wait_ge(sim_ps, i + 1)
                    act.activation(simT[:, :, :], ps_sim, ACT.Relu, scale=1.0 / SEQ).then_inc(sim_done, 1)
                if not absent(r):
                    act.wait_ge(u_rows_done, r + 1)
                    act.activation(row_b[:, :, 0:D], row_a[:, :, 0:D], ACT.Copy).then_inc(row_b_done, 1)
                    act.wait_ge(uT_ps, r + 1)
                    act.activation(uT[:, :, :], ps_uT, ACT.Copy).then_inc(uT_done, 1)
                if not absent(i):
                    act.wait_ge(gate_ps, i + 1)
                    act.activation(gateT[:, :, :], ps_gate, ACT.Silu).then_inc(gate_done, 1)
                if not absent(i + 1):
                    act.wait_ge(nT_ps, i + 2)
                    for k in range(NKC):
                        last = act.activation(nT[0:KC, k, :], ps_nT[:, k, :], ACT.Identity,
                                              bias=ln_sb[:, 1, k:k + 1], scale=ln_sb[:, 0, k:k + 1])
                    last.then_inc(nT_done, 1)
                    act.wait_ge(z_ps, i + 2)
                    act.activation(zT[:, :], ps_z, ACT.Silu).then_inc(z_done, 1)
                if not absent(r):
                    act.wait_ge(diff_done, r + 1)
                    act.activation(tanh_d[:, :], diff[:, :], ACT.Tanh, scale=0.5).then_inc(tanh_done, 1)

            pipeline(act, attn_step, **ATTN)

            with act.Fori(0, MOE_TILES) as j:
                act.wait_ge(h_ps, j + 1)
                act.activation(h_sb[:, :].rearrange("p (b n) -> p b n", b=2), ps_h, ACT.Gelu).then_inc(h_done, 1)

            act.wait_ge(added, 16 * MOE_TILES)
            act.wait_ge(stored, 16 * (IMAGES + 1))

        @block.vector
        def _(dve):
            chain = Chain(dve, dve_self)
            INV_GROUP = 1.0 / (SEQ * GC)

            def token_moments(i):
                for t in range(HALVES):
                    last = dve.bn_stats(stats[:, t, :], X[:, ds(i * HALVES + t, 1), :])
                dve.drain()
                for t in range(HALVES):
                    last = dve.bn_aggr(mom[:, t, :], stats[:, t, :])
                chain.link(last)

            def rsqrt(y, v, neg_half_v, work):
                chain.link(dve.tensor_scalar(y.bitcast(i32), v.bitcast(i32), -0.5, float(0x5F3759DF),
                                             ALU.mult, ALU.add))
                for n in range(3):
                    chain.link(dve.tensor_tensor(work, neg_half_v, y, ALU.mult))
                    chain.link(dve.tensor_tensor(work, work, y, ALU.mult))
                    last = dve.scalar_tensor_tensor(y, work, 1.5, y, ALU.add, ALU.mult)
                    if n < 2:
                        chain.link(last)
                return last

            def conv_step(i):
                if not absent(i + 3):
                    dve.wait_ge(gsum_done, i + 4)
                    wait(dve, xc_done, i + 3)
                    dve.tensor_scalar(gmean[:, :], ps_gsum, INV_GROUP, None, ALU.mult).then_inc(gmean_done, 1)
                if not absent(i - 1):
                    dve.wait_ge(conv_ps, i)
                    dve.tensor_tensor(X[:, tiles(i - 1), :], X[:, tiles(i - 1), :], ps_conv,
                                      ALU.add).then_inc(conv_read, 1)
                if not absent(i + 2):
                    dve.wait_ge(gsq_done, i + 3)
                    dve.tensor_scalar(gneg[:, :], ps_gsq, -0.5 * INV_GROUP, -0.5 * LN_EPS, ALU.mult, ALU.add)
                    chain.link(dve.tensor_scalar(gvar[:, :], ps_gsq, INV_GROUP, LN_EPS, ALU.mult, ALU.add))
                    wait(dve, xn_done, i + 2)
                    chain.mark(dve.tensor_scalar(grs[:, :].bitcast(i32), gvar[:, :].bitcast(i32), -0.5,
                                                 float(0x5F3759DF), ALU.mult, ALU.add))
                if not absent(i - 1):
                    wait_alone(dve, conv_read, i, ld_const)
                    dve.bn_stats(stats[:, 0, :], X[:, ds((i - 1) * HALVES, 1), :])
                if not absent(i + 2):
                    chain.wait()
                    chain.mark(dve.tensor_tensor(newton[:, :], gneg[:, :], grs[:, :], ALU.mult))
                if not absent(i - 1):
                    dve.bn_stats(stats[:, 1, :], X[:, ds((i - 1) * HALVES + 1, 1), :])
                if not absent(i + 2):
                    chain.wait()
                    chain.mark(dve.tensor_tensor(newton[:, :], newton[:, :], grs[:, :], ALU.mult))
                if not absent(i + 4):
                    dve.wait_ge(ld_x, (i + 5) * 16)
                    wait(dve, gsum_done, i + 4)
                    dve.tensor_reduce(gsum[:, :], grouped(X[:, tiles(i + 4), :]).rearrange("p t g c -> p g t c"),
                                      AX.XY, ALU.add).then_inc(gsum_in, 1)
                if not absent(i + 2):
                    chain.wait()
                    last = dve.scalar_tensor_tensor(grs[:, :], newton[:, :], 1.5, grs[:, :], ALU.add, ALU.mult)
                    for n in range(2):
                        chain.link(last)
                        chain.link(dve.tensor_tensor(newton[:, :], gneg[:, :], grs[:, :], ALU.mult))
                        chain.link(dve.tensor_tensor(newton[:, :], newton[:, :], grs[:, :], ALU.mult))
                        last = dve.scalar_tensor_tensor(grs[:, :], newton[:, :], 1.5, grs[:, :], ALU.add, ALU.mult)
                    last.then_inc(grs_done, 1)
                if not absent(i - 1):
                    dve.drain()
                    for t in range(HALVES):
                        last = dve.bn_aggr(mom[:, t, :], stats[:, t, :])
                    chain.mark(last)
                if not absent(i + 3):
                    dve.wait_ge(sq_done, i + 4)
                    wait(dve, gsq_done, i + 3)
                    dve.tensor_reduce(gsq[:, :], grouped(xsq[:, :, :]).rearrange("p t g c -> p g t c"),
                                      AX.XY, ALU.add).then_inc(gsq_in, 1)
                if not absent(i - 1):
                    chain.wait()
                    chain.link(dve.tensor_copy(moments[:, tiles(i - 1), :], mom[:, :, :]))

            dve.wait_ge(ld_const, 16)
            pipeline(dve, conv_step, **CONV, chain=chain, per=12)

            mean, var = moments[:, :, 0], moments[:, :, 1]
            dve.engine_nop().then_inc(mom_var, 1)
            dve.wait_ge(mom_std, 1)
            chain.link(dve.reciprocal(rs1[:, :], rs1[:, :]))
            chain.link(dve.tensor_tensor(tmp32[:, :], var, rs1[:, :], ALU.mult))
            dve.tensor_tensor(tmp32[:, :], tmp32[:, :], rs1[:, :], ALU.mult).then_inc(mom2_var, 1)
            dve.tensor_scalar(r_scale[:, :], rs1[:, :], 1.0, None, ALU.add)
            dve.scalar_tensor_tensor(r_bias[:, :], mean, -1.0, rs1[:, :], ALU.mult, ALU.mult)
            dve.wait_ge(mom2_std, 1)
            chain.link(dve.reciprocal(n_scale[:, :], n_bias[:, :]))
            chain.link(dve.tensor_tensor(n_scale[:, :], n_scale[:, :], rs1[:, :], ALU.mult))
            dve.scalar_tensor_tensor(n_bias[:, :], mean, -1.0, n_scale[:, :], ALU.mult,
                                     ALU.mult).then_inc(scales_done, 1)

            def query_key(i):
                dve.wait_ge(z_done, i + 1)
                for n, dst in enumerate((qT, kT)):
                    last = dve.tensor_scalar(dst[:, :], zT[:, :], gb_sb[:, n:n + 1], gb_sb[:, 2 + n:3 + n],
                                             ALU.mult, ALU.add)
                last.then_inc(qk_done, 1)

            def choose(r):
                dve.wait_ge(logits_ps, r + 1)
                chain.link(dve.tensor_copy(logits[:, :, :], ps_logits))
                shape = (P, HALVES, EXPERTS, EXPERTS)
                other = logits[:, :, :].unsqueeze(2).broadcast_to(shape)
                own = logits[:, :, :].unsqueeze(3).broadcast_to(shape)
                dve.tensor_tensor(above[:, :, :, :], other, own, ALU.is_gt)
                chain.link(dve.tensor_tensor(equal[:, :, :, :], other, own, ALU.is_equal))
                lower = K("lower").rearrange("p (a b) -> p a b", b=EXPERTS).unsqueeze(1).broadcast_to(shape)
                chain.link(dve.tensor_tensor(equal[:, :, :, :], equal[:, :, :, :], lower, ALU.mult))
                chain.link(dve.tensor_tensor(above[:, :, :, :], above[:, :, :, :], equal[:, :, :, :], ALU.add))
                chain.link(dve.tensor_reduce(rank[:, :, :], above[:, :, :, :], AX.X, ALU.add))
                for c in range(2):
                    last = dve.tensor_scalar(chosen[:, c, :], rank[:, :, :].rearrange("p t e -> p (t e)"),
                                             float(c), None, ALU.is_equal)
                chain.link(last)
                by_expert = chosen[:, :, :].rearrange("p c (t e) -> p e c t", e=EXPERTS)
                dve.tensor_reduce(in_row[:, :], by_expert, AX.XY, ALU.add).then_inc(in_row_done, 1)
                dve.tensor_tensor(in_first[:, :], chosen[:, 0, 0:EXPERTS], chosen[:, 1, 0:EXPERTS], ALU.add)
                both = logits[:, :, :].rearrange("p t e -> p (t e)").unsqueeze(1).broadcast_to(
                    (P, 2, HALVES * EXPERTS))
                chain.link(dve.tensor_tensor(picked[:, :, :], chosen[:, :, :], both, ALU.mult))
                chain.link(dve.tensor_reduce(top[:, :, :], picked[:, :, :].rearrange(
                    "p c (t e) -> p c t e", e=EXPERTS), AX.X, ALU.add))
                dve.tensor_tensor(diff[:, :], top[:, 0, :], top[:, 1, :], ALU.subtract).then_inc(diff_done, 1)

            def place(r):
                dve.wait_ge(prefix_ps, r + 1)
                chain.link(dve.tensor_tensor(slot[:, 0, :], list_at[:, :], ps_rows_before, ALU.add))
                dve.tensor_tensor(slot[:, 1, :], slot[:, 0, :], in_first[:, :], ALU.add)
                ins = dve.tensor_tensor(list_at[:, :], list_at[:, :], ps_rows_all, ALU.add)
                ins.then_inc(prefix_read, 1)
                dve.wait_ge(prefix_read, r + 1)
                both = slot[:, :, :].rearrange("p t e -> p (t e)").unsqueeze(1).broadcast_to(
                    (P, 2, HALVES * EXPERTS))
                chain.link(dve.tensor_tensor(picked[:, :, :], chosen[:, :, :], both, ALU.mult))
                with nc.allow_low_precision(reason="whole numbers below 2**24"):
                    dve.tensor_reduce(slots[:, :, :], picked[:, :, :].rearrange("p c (t e) -> p c t e", e=EXPERTS),
                                      AX.X, ALU.add).then_inc(slots_done, 1)
                dve.wait_ge(tanh_done, r + 1)
                for rows, sign in ((row_a, 0.5), (row_b, -0.5)):
                    last = dve.tensor_scalar(rows[:, :, D + 1:D + 2], tanh_d[:, :].unsqueeze(2), sign, 0.5,
                                             ALU.mult, ALU.add)
                last.then_inc(row_a_done, 1)

            def attn_step(i):
                r = i - 1
                if not absent(i):
                    dve.wait_ge(sim_done, i + 1)
                    dve.tensor_tensor(attnT[:, :, :], simT[:, :, :], simT[:, :, :], ALU.mult).then_inc(attn_done, 1)
                if not absent(r):
                    choose(r)
                if not absent(i):
                    dve.wait_ge(gate_done, i + 1)
                    for k, (lo, hi) in enumerate(((0, 2), (2, 3))):
                        dve.wait_ge(av_ps, 2 * i + 1 + k)
                        dve.tensor_tensor(gatedT[:, lo:hi, :], ps_av[:, lo:hi, :], gateT[:, lo:hi, :],
                                          ALU.mult).then_inc(gated_done, 1)
                if not absent(i + 1):
                    query_key(i + 1)
                if not absent(r):
                    place(r)
                if not absent(i):
                    dve.wait_ge(out_ps, i + 1)
                    dve.wait_ge(base_done, i + 1)
                    ins = dve.tensor_tensor(X[:, tiles(i), :], X[:, tiles(i), :], ps_out, ALU.add)
                    ins.then_inc(t2_done, 1)
                    wait_alone(dve, t2_done, i + 1, ld_const)
                    token_moments(i)
                    dve.tensor_scalar(u_neg[:, :], mom[:, :, 1], -0.5, -0.5 * LN_EPS, ALU.mult, ALU.add)
                    chain.link(dve.tensor_scalar(u_var[:, :], mom[:, :, 1], LN_EPS, None, ALU.add))
                    chain.link(rsqrt(u_scale[:, :], u_var[:, :], u_neg[:, :], newton[:, 0:HALVES]))
                    chain.link(dve.scalar_tensor_tensor(u_bias[:, :], mom[:, :, 0], -1.0, u_scale[:, :],
                                                        ALU.mult, ALU.mult))
                    wait(dve, scattered, i * (16 * 2 * HALVES))
                    for t in range(HALVES):
                        last = dve.tensor_scalar(row_a[:, t, 0:D], X[:, ds(i * HALVES + t, 1), :],
                                                 u_scale[:, t:t + 1], u_bias[:, t:t + 1], ALU.mult, ALU.add)
                    last.then_inc(u_rows_done, 1)

            dve.wait_ge(ld_attn, 16 * 13)
            dve.wait_ge(pads_ready, 1)
            pipeline(dve, attn_step, **ATTN, chain=chain, per=23)

            n_regions = (P, EXPERTS, TOKENS // P)
            n_all = (P, MOE_TILES, EXPERTS)
            dve.tensor_copy(list_end[:, :], list_at[:, :])
            chain.link(dve.tensor_tensor(n_list[:, :], list_at[:, :], K("list_base"), ALU.subtract))
            chain.link(dve.tensor_tensor(over[:, :, :], n_list[:, :].unsqueeze(2).broadcast_to(n_regions),
                                         K("tile_rows").unsqueeze(1).broadcast_to(n_regions), ALU.is_gt))
            chain.link(dve.tensor_reduce(n_tiles[:, :], over[:, :, :], AX.X, ALU.add))
            chain.link(dve.tensor_tensor_scan(t_end[:, :], K("ones")[:, 0:EXPERTS], n_tiles[:, :], 0.0,
                                              ALU.mult, ALU.add))
            chain.link(dve.tensor_tensor(t_start[:, :], t_end[:, :], n_tiles[:, :], ALU.subtract))
            tile_no = K("tile_no").unsqueeze(2).broadcast_to(n_all)

            def per_tile(ap):
                return ap.unsqueeze(1).broadcast_to(n_all)

            dve.scalar_tensor_tensor(base[:, :], t_start[:, :], -float(P), K("list_base"), ALU.mult, ALU.add)
            dve.tensor_tensor(started[:, :, :], tile_no, per_tile(t_start[:, :]), ALU.is_ge)
            chain.link(dve.tensor_tensor(ended[:, :, :], tile_no, per_tile(t_end[:, :]), ALU.is_ge))
            chain.link(dve.tensor_reduce(tile_f[:, :], ended[:, :, :], AX.X, ALU.add))
            dve.tensor_scalar(tile_expert[:, :], tile_f[:, :], float(EXPERTS - 1), None, ALU.min)
            dve.tensor_tensor(started[:, :, :], started[:, :, :], ended[:, :, :], ALU.subtract)
            chain.link(dve.scalar_tensor_tensor(rows_at[:, :, :], tile_no, float(P), per_tile(base[:, :]),
                                                ALU.mult, ALU.add))
            chain.link(dve.tensor_scalar(rows_at[:, :, :], rows_at[:, :, :], -float(SPARE), None, ALU.add))
            chain.link(dve.tensor_tensor(rows_at[:, :, :], rows_at[:, :, :], started[:, :, :], ALU.mult))
            chain.link(dve.tensor_reduce(tile_f[:, :], rows_at[:, :, :], AX.X, ALU.add))
            dve.tensor_scalar(tile_row[:, :], tile_f[:, :], float(SPARE), None,
                              ALU.add).then_inc(tiles_done, 1)
            dve.wait_ge(tiles_done, 1)

            def moe_step(j):
                if not absent(j + 1, MOE_TILES):
                    dve.wait_ge(sT_ps, j + 2)
                    dve.tensor_copy(sT[0:KC, :, :], ps_sT).then_inc(sT_done, 1)
                    dve.tensor_copy(meta[:, ds(j + 1, 1), :],
                                    slot_rows[:, D:D + 2].bitcast(i32).unsqueeze(1)).then_inc(meta_done, 1)
                if not absent(j - 1, MOE_TILES):
                    p = j - 1
                    e = dve.value_load(tile_expert[0:1, ds(p, 1)], min_val=0, max_val=EXPERTS - 1)
                    dve.wait_ge(y_ps, p + 1)
                    wait(dve, added, p * 16)
                    dve.tensor_tensor(y_sb[:, :].unsqueeze(1), ps_y.unsqueeze(1), b_o_sb[:, ds(e, 1), :],
                                      ALU.add).then_inc(y_read, 1)
                    dve.tensor_copy(y_id[:, :].unsqueeze(1), meta[:, ds(p, 1), 0:1])
                    dve.wait_ge(y_read, p + 1)
                    w = meta[:, ds(p, 1), 1:2].bitcast(f32)
                    dve.tensor_scalar(y_sb[:, :], y_sb[:, :], w.rearrange("p a b -> p (a b)"), None,
                                      ALU.mult).then_inc(y_done, 1)
                if not absent(j, MOE_TILES):
                    for k in range(2):
                        dve.wait_ge(hT_ps, 2 * j + 1 + k)
                        dve.tensor_copy(hT[:, k * FF // 2:(k + 1) * FF // 2], ps_hT[:, k, :]).then_inc(hT_done, 1)

            pipeline(dve, moe_step, **MOE)

        @block.tensor
        def _(pe):
            pe.wait_ge(ld_const, 16)
            pe.wait_ge(ld_w1, 32)
            pe.wait_ge(ones_set, 4)

            def mm(dst, lhsT, rhs, start=True, stop=True):
                return pe.matmul(dst, lhsT, rhs, start=start, stop=stop)

            def conv_step(i):
                if not absent(i):
                    pe.wait_ge(coef_done, i + 1)
                    for f in range(NFC):
                        for k in range(NKC):
                            rows = KC + (k == NKC - 1)
                            last = mm(ps_mix[:, f, :], coef[0:rows, k, f * FCH:(f + 1) * FCH],
                                      w1_sb[0:rows, k, :], k == 0, k == NKC - 1)
                    last.then_inc(mix_ps, 1)
                if not absent(i + 1):
                    pe.wait_ge(xn_done, i + 2)
                    for k in range(NKC):
                        ch = slice(k * KC, (k + 1) * KC)
                        mm(ps_coef[:, k, 0:2 * FCH], xn[:, 0, ch], K("fwd0"), True, False)
                        mm(ps_coef[:, k, FCH:2 * FCH], xn[:, 1, ch], K("fwd1")[:, 0:FCH], False, True)
                        last = mm(ps_coef[:, k, 2 * FCH:3 * FCH], xn[:, 1, ch], K("fwd1")[:, FCH:2 * FCH])
                    last.then_inc(coef_ps, 1)
                if not absent(i + 4):
                    pe.wait_ge(gsum_in, i + 5)
                    wait(pe, gmean_done, i + 4)
                    mm(ps_gsum, K("ones"), gsum[:, :]).then_inc(gsum_done, 1)
                if not absent(i):
                    pe.wait_ge(mix_done, i + 1)
                    wait(pe, conv_read, i)
                    mm(ps_conv[:, 0, :], K("inv0a", FCH), mixed[:, 0, :], True, False)
                    mm(ps_conv[:, 0, :], K("inv0b", FCH), mixed[:, 1, :], False, True)
                    mm(ps_conv[:, 1, :], K("inv1b", FCH), mixed[:, 1, :], True, False)
                    mm(ps_conv[:, 1, :], K("inv1c", FCH), mixed[:, 2, :], False, True).then_inc(conv_ps, 1)
                if not absent(i + 3):
                    pe.wait_ge(gsq_in, i + 4)
                    wait(pe, grs_done, i + 3)
                    mm(ps_gsq, K("ones"), gsq[:, :]).then_inc(gsq_done, 1)

            pipeline(pe, conv_step, **CONV)
            pe.wait_ge(ld_attn, 16 * 13)

            def z_product(i):
                pe.wait_ge(nT_done, i + 1)
                for k in range(NKC):
                    rows = KC + (k == NKC - 1)
                    last = mm(ps_z, w_qk_sb[0:rows, k, :], nT[0:rows, k, :], k == 0, k == NKC - 1)
                last.then_inc(z_ps, 1)

            def gates(c):
                for k in range(NKC):
                    rows = KC + (k == NKC - 1)
                    last = mm(ps_gate[:, c, :], w_hid_sb[0:rows, k, HID + c * P:HID + (c + 1) * P],
                              nT[0:rows, k, :], k == 0, k == NKC - 1)
                return last

            def attn_step(i):
                r = i - 1
                if not absent(i):
                    for t in range(HALVES):
                        for k in range(NKC):
                            rows = KC + (k == NKC - 1)
                            last = mm(ps_v[:, t, :], nT[0:rows, k, t * P:(t + 1) * P], w_hid_sb[0:rows, k, 0:HID],
                                      k == 0, k == NKC - 1)
                    last.then_inc(v_ps, 1)
                if not absent(i):
                    pe.wait_ge(qk_done, i + 1)
                    for t in range(HALVES):
                        last = mm(ps_sim[:, t, :], kT[:, t * P:(t + 1) * P], qT[:, :])
                    last.then_inc(sim_ps, 1)
                    gates(0)
                    gates(1)
                    gates(2).then_inc(gate_ps, 1)
                if not absent(r):
                    pe.wait_ge(u_rows_done, r + 1)
                    wait(pe, prefix_read, r)
                    for t in range(HALVES):
                        for k in range(NKC):
                            last = pe.transpose(ps_uT[:, k, t * P:(t + 1) * P], row_a[:, t, k * KC:(k + 1) * KC],
                                                K("ident"))
                    last.then_inc(uT_ps, 1)
                if not absent(i + 1):
                    pe.wait_ge(normed_done, i + 2)
                    for t in range(HALVES):
                        for k in range(NKC):
                            last = pe.transpose(ps_nT[:, k, t * P:(t + 1) * P], normed[:, t, k * KC:(k + 1) * KC],
                                                K("ident"))
                    last.then_inc(nT_ps, 1)
                if not absent(r):
                    pe.wait_ge(uT_done, r + 1)
                    for t in range(HALVES):
                        for k in range(NKC):
                            last = mm(ps_logits[:, t, :], uT[:, k, t * P:(t + 1) * P], w_r_sb[:, k, :],
                                      k == 0, k == NKC - 1)
                    last.then_inc(logits_ps, 1)
                if not absent(i):
                    pe.wait_ge(v_done, i + 1)
                    pe.wait_ge(attn_done, i + 1)
                    for c in range(HID // P):
                        for t in range(HALVES):
                            last = mm(ps_av[:, c, :], v_sb[:, t, c * P:(c + 1) * P], attnT[:, t, :],
                                      t == 0, t == HALVES - 1)
                        if c >= 1:
                            last.then_inc(av_ps, 1)
                if not absent(i + 1):
                    z_product(i + 1)
                if not absent(r):
                    pe.wait_ge(in_row_done, r + 1)
                    mm(ps_rows_before, K("before"), in_row[:, :])
                    mm(ps_rows_all, K("ones"), in_row[:, :]).then_inc(prefix_ps, 1)
                if not absent(i):
                    wait(pe, t2_done, i)
                    pe.wait_ge(gated_done, 2 * i + 2)
                    for t in range(HALVES):
                        for c in range(HID // P):
                            last = mm(ps_out[:, t, :], gatedT[:, c, t * P:(t + 1) * P], w_out_sb[:, c, :],
                                      c == 0, c == HID // P - 1)
                    last.then_inc(out_ps, 1)

            pipeline(pe, attn_step, **ATTN)

            pe.wait_ge(ld_exp, 32)
            pe.wait_ge(tiles_done, 1)

            def moe_step(j):
                if not absent(j, MOE_TILES):
                    e = pe.value_load(tile_expert[0:1, ds(j, 1)], min_val=0, max_val=EXPERTS - 1)
                    pe.wait_ge(sT_done, j + 1)
                    for b in range(2):
                        for k in range(NKC):
                            rows = KC + (k == NKC - 1)
                            last = mm(ps_h[:, b, :], sT[0:rows, k, :],
                                      w_i_sb[0:rows, ds(e, 1), k, b * FF // 2:(b + 1) * FF // 2],
                                      k == 0, k == NKC - 1)
                    last.then_inc(h_ps, 1)
                if not absent(j + 1, MOE_TILES):
                    pe.wait_ge(rows_in, (j + 2) * 16)
                    for k in range(NKC):
                        last = pe.transpose(ps_sT[:, k, :], slot_rows[:, k * KC:(k + 1) * KC], K("ident"))
                    last.then_inc(sT_ps, 1)
                if not absent(j - 1, MOE_TILES):
                    p = j - 1
                    e = pe.value_load(tile_expert[0:1, ds(p, 1)], min_val=0, max_val=EXPERTS - 1)
                    pe.wait_ge(hT_done, 2 * p + 2)
                    wait(pe, y_read, p)
                    for f in range(FCHUNKS):
                        last = mm(ps_y, hT[:, f * P:(f + 1) * P], w_o_sb[:, ds(e, 1), f, :], f == 0,
                                  f == FCHUNKS - 1)
                    last.then_inc(y_ps, 1)
                if not absent(j, MOE_TILES):
                    pe.wait_ge(h_done, j + 1)
                    for f in range(FCHUNKS):
                        b, c = divmod(f, FCHUNKS // 2)
                        last = pe.transpose(ps_hT[:, b, c * P:(c + 1) * P], h_sb[:, f * P:(f + 1) * P], K("ident"))
                        if c == FCHUNKS // 2 - 1:
                            last.then_inc(hT_ps, 1)

            pipeline(pe, moe_step, **MOE)


def kernel(x, L0_conv_W1, L0_conv_b1, L1_attn_ln_w, L1_attn_ln_b, L1_attn_W_hidden, L1_attn_b_hidden,
           L1_attn_W_qk, L1_attn_b_qk, L1_attn_gamma, L1_attn_beta, L1_attn_W_out, L1_attn_b_out,
           L1_ffn_Wr, L1_ffn_Wi, L1_ffn_bi, L1_ffn_Wo, L1_ffn_bo):
    import concourse.bacc as bacc
    from concourse.bass_utils import run_bass_kernel_spmd

    def packed(w, rows):
        w = np.asarray(w)
        w = w.reshape(*w.shape[:-1], w.shape[-1] // rows, rows)
        w = np.swapaxes(w, -3, -2)
        return np.ascontiguousarray(np.moveaxis(w, -1, 0))

    def columns(v):
        return np.ascontiguousarray(np.asarray(v).reshape(NKC, KC).T)

    arrays = {
        "x": np.asarray(x).reshape(TOKENS, D), "consts": shape_constants(),
        "w1": packed(L0_conv_W1, KC), "b1": np.asarray(L0_conv_b1).reshape(1, D),
        "ln_w": columns(L1_attn_ln_w), "ln_b": columns(L1_attn_ln_b),
        "w_hid": packed(L1_attn_W_hidden, KC), "b_hid": np.asarray(L1_attn_b_hidden).reshape(1, 2 * HID),
        "w_qk": packed(L1_attn_W_qk, KC), "b_qk": np.asarray(L1_attn_b_qk).reshape(1, QK),
        "gamma": np.ascontiguousarray(np.asarray(L1_attn_gamma).T),
        "beta": np.ascontiguousarray(np.asarray(L1_attn_beta).T),
        "w_out": packed(L1_attn_W_out, P), "b_out": np.asarray(L1_attn_b_out),
        "w_r": packed(L1_ffn_Wr, KC),
        "w_i": packed(L1_ffn_Wi, KC), "b_i": np.asarray(L1_ffn_bi).reshape(1, EXPERTS, FF),
        "w_o": packed(L1_ffn_Wo, P), "b_o": np.asarray(L1_ffn_bo),
    }
    nc = bacc.Bacc("TRN2", target_bir_lowering=False, num_devices=1)
    aps = [nc.dram_tensor(f"in_{n}", a.shape, mybir.dt.from_np(a.dtype), kind="ExternalInput").ap()
           for n, a in arrays.items()]
    out = nc.dram_tensor("out_rows", (TOKENS + P, D), mybir.dt.float32, kind="ExternalOutput").ap()
    names = dict(zip(arrays, aps))
    build(nc, **names, out=out)
    r = run_bass_kernel_spmd(nc, [{f"in_{n}": a for n, a in arrays.items()}], core_ids=[0])
    return r.results[0]["out_rows"][:TOKENS].reshape(IMAGES, SIDE, SIDE, D)
```

```python
from contextlib import ExitStack

import numpy as np
import concourse.bass as bass
from concourse import mybir

IMAGES, SIDE, D = 16, 16, 192
TOKENS = IMAGES * SIDE * SIDE
SEQ = SIDE * SIDE
P = 128
HALVES = SEQ // P
GROUPS = 32
GC = D // GROUPS
BLOCK = 3
BROWS = -(-SIDE // BLOCK)
FCH = 2 * BROWS * BLOCK * BLOCK
NFC = BROWS // 2
KC = 96
NKC = D // KC
HID = 2 * D
QK = 32
EXPERTS, FF = 8, 768
FCHUNKS = FF // P
HALF = FF // 2
SLICE = NKC * HALF
NSLICE = NKC + EXPERTS * FF // HALF
assert SLICE == 2 * HID
SHARED = FCHUNKS // HALVES
LOADED_EARLY = IMAGES // SHARED
REGION = TOKENS + P
SPARE = EXPERTS * REGION
ROW = D + 2
MOE_TILES = (2 * TOKENS + EXPERTS * (P - 1)) // P
FIRST_TILES = 3
assert FIRST_TILES % 2 == 1 and MOE_TILES % 2 == 1
assert 2 * (TOKENS - 2 * SEQ) - EXPERTS * (P - 1) > FIRST_TILES * P
LN_EPS = 1e-5
SCALED = IMAGES - 3
X_GROUPS = (1, 1, 2, 4, 8)
assert sum(X_GROUPS) == IMAGES

_WIDTHS = [("ident", P), ("ones", P), ("before", P), ("fwd0", 2 * FCH), ("fwd1", 2 * FCH),
           ("inv0a", P), ("inv0b", P), ("inv1b", P), ("inv1c", P), ("lower", EXPERTS * EXPERTS),
           ("list_base", EXPERTS), ("tile_rows", TOKENS // P), ("tile_no", 1), ("tile_at", 1),
           ("ids", HALVES), ("pad_id", 1)]
CONST_AT, CONST_W = {}, 0
for _n, _w in _WIDTHS:
    CONST_AT[_n] = (CONST_W, CONST_W + _w)
    CONST_W += _w


def shape_constants():
    c = np.zeros((P, CONST_W), np.float32)

    def put(name, a):
        lo, _ = CONST_AT[name]
        c[:a.shape[0], lo:lo + a.shape[1]] = a

    k, n = np.arange(BLOCK)[:, None], np.arange(BLOCK)[None, :]
    dct = np.cos(np.pi / BLOCK * (n + 0.5) * k) * np.where(k == 0, np.sqrt(1 / BLOCK), np.sqrt(2 / BLOCK))
    fwd = np.zeros((SEQ, NFC * FCH))
    inv = np.zeros((NFC * FCH, SEQ))
    for bh in range(BROWS):
        for bw in range(BROWS):
            for a in range(BLOCK):
                for b in range(BLOCK):
                    f = ((bh * BROWS + bw) * BLOCK + a) * BLOCK + b
                    for r in range(BLOCK):
                        for s in range(BLOCK):
                            h, w = bh * BLOCK + r, bw * BLOCK + s
                            fwd[min(h, SIDE - 1) * SIDE + min(w, SIDE - 1), f] += dct[a, r] * dct[b, s]
                            if h < SIDE and w < SIDE:
                                inv[f, h * SIDE + w] = dct[a, r] * dct[b, s]
    assert not fwd[:P, 2 * FCH:].any() and not fwd[P:, :FCH].any()
    put("ident", np.eye(P))
    put("ones", np.ones((P, P)))
    put("before", np.triu(np.ones((P, P)), 1))
    put("fwd0", fwd[:P, :2 * FCH])
    put("fwd1", fwd[P:, FCH:])
    put("inv0a", inv[:FCH, :P])
    put("inv0b", inv[FCH:2 * FCH, :P])
    put("inv1b", inv[FCH:2 * FCH, P:])
    put("inv1c", inv[2 * FCH:, P:])
    assert not inv[:FCH, P:].any() and not inv[2 * FCH:, :P].any()
    every = np.ones((P, 1))
    put("lower", every * np.tril(np.ones((EXPERTS, EXPERTS)), -1).reshape(1, -1))
    put("list_base", every * (np.arange(EXPERTS) * REGION)[None])
    put("tile_rows", every * (np.arange(TOKENS // P) * P)[None])
    put("tile_no", np.arange(P)[:, None])
    put("tile_at", np.arange(P)[:, None] * P - SPARE)
    put("ids", np.arange(P)[:, None] + P * np.arange(HALVES)[None] - SEQ)
    put("pad_id", TOKENS + np.arange(P)[:, None])
    return c


def wait(eng, sem, value):
    if isinstance(value, int) and value <= 0:
        return
    eng.wait_ge(sem, value)


def wait_alone(eng, sem, value, held):
    eng.wait_ge(held, 16)
    eng.wait_ge(sem, value)


class Chain:

    def __init__(self, eng, sem):
        self.eng, self.sem, self.count, self.extra = eng, sem, 0, 0

    def mark(self, ins):
        ins.then_inc(self.sem, 1)
        self.count += 1

    def wait(self):
        self.eng.wait_ge(self.sem, self.count + self.extra)

    def link(self, ins):
        self.mark(ins)
        self.wait()


def pipeline(eng, step, first, last, ahead, behind, unroll=1, parity=False, chain=None, per=0):
    assert not parity or unroll == 2

    def run(i, odd):
        step(i, odd) if parity else step(i)

    n = last + 1 - behind
    lo, hi = behind + 1, n - ahead
    hi -= (hi - lo) % unroll
    for i in range(first, lo):
        run(i, i % 2)
    with eng.Fori(lo, hi - unroll + 1, unroll) as i:
        if chain:
            start = chain.count
            chain.extra = (i - lo) * per
        for u in range(unroll):
            run(i + u if u else i, (lo + u) % 2)
    if chain:
        assert chain.count - start == per * unroll, (chain.count - start, per)
        chain.count = start + per * (hi - lo)
        chain.extra = 0
    for i in range(hi, last + 1):
        run(i, i % 2)


def build(nc, x, consts, w1, b1, ln_w, ln_b, split_w, w_qk, gamma, beta, w_out, b_out, w_r,
          w_o, b_o, out):
    f32, f32r, i32, bf16 = mybir.dt.float32, mybir.dt.float32r, mybir.dt.int32, mybir.dt.bfloat16
    ALU, ACT, AX = mybir.AluOpType, mybir.ActivationFunctionType, mybir.AxisListType
    ds = bass.ds

    lists = nc.dram_tensor("lists", (SPARE + P, ROW), f32, kind="Internal").ap()

    ctx = ExitStack()
    with ctx:
        def sb(name, shape, dt=f32):
            return ctx.enter_context(nc.sbuf_tensor(name, shape, dt))

        def sem(name):
            return ctx.enter_context(nc.semaphore(name))

        const = sb("const", [P, CONST_W])

        def K(name, rows=P):
            lo, hi = CONST_AT[name]
            return const[0:rows, lo:hi]

        w_o_sb = sb("w_o_sb", [P, EXPERTS, FCHUNKS, D])
        early = w_o_sb[:, :, :, :].rearrange("p e f c -> p (e f c)")
        X = early[:, 0:IMAGES * HALVES * D].rearrange("p (n c) -> p n c", c=D)
        early_at = [IMAGES * HALVES * D]

        def early_buffer(n, width):
            at = early_at[0]
            early_at[0] += n * width
            return early[:, at:at + n * width].rearrange("p (n w) -> p n w", w=width)

        moments = sb("moments", [P, IMAGES * HALVES, 2])

        w1_sb = sb("w1_sb", [KC + 1, NKC, D])
        gsum = sb("gsum", [P, GROUPS])
        gsq = sb("gsq", [P, GROUPS])
        gmean = sb("gmean", [P, GROUPS])
        gvar = sb("gvar", [P, GROUPS])
        grs = sb("grs", [P, GROUPS])
        gneg = sb("gneg", [P, GROUPS])
        newton = sb("newton", [P, GROUPS])
        xsq = sb("xsq", [P, HALVES, D])
        xc = sb("xc", [P, 2, HALVES, D])
        xn = sb("xn", [P, HALVES, D])
        coef = sb("coef", [KC + 1, NKC, NFC * FCH])
        mixed = sb("mixed", [FCH, NFC, D])
        stats = sb("stats", [P, HALVES, 6])
        mom = sb("mom", [P, HALVES, 2])

        w_qk_sb = sb("w_qk_sb", [KC + 1, NKC, QK])
        w_qk_hi = sb("w_qk_hi", [KC + 1, NKC, QK], f32r)
        w_qk_lo = sb("w_qk_lo", [KC + 1, NKC, QK], f32r)
        w_out_sb = sb("w_out_sb", [P, HID // P, D])
        ln_sb = sb("ln_sb", [KC, 2, NKC])
        gb_sb = sb("gb_sb", [QK, 4])
        b_out_sb = sb("b_out_sb", [P, D])
        w_r_sb = sb("w_r_sb", [KC, NKC, EXPERTS])
        rs1 = sb("rs1", [P, IMAGES * HALVES])
        ln_var = sb("ln_var", [P, IMAGES * HALVES])
        ln_neg = sb("ln_neg", [P, IMAGES * HALVES])
        ln_work = sb("ln_work", [P, IMAGES * HALVES])
        n_scale = sb("n_scale", [P, IMAGES * HALVES])
        n_bias = sb("n_bias", [P, IMAGES * HALVES])
        r_scale = sb("r_scale", [P, IMAGES * HALVES])
        r_bias = sb("r_bias", [P, IMAGES * HALVES])
        normed = xn
        nT = sb("nT", [KC, NKC, SEQ])
        nT_hi = sb("nT_hi", [KC + 1, NKC, SEQ], f32r)
        nT_lo = sb("nT_lo", [KC + 1, NKC, SEQ], f32r)
        zT, qT, kT = (xc[0:QK, :, :, :].rearrange("p a t c -> p (a t c)")[:, n * SEQ:(n + 1) * SEQ] for n in range(3))
        v_sb = early_buffer(HALVES, HID)
        gateT = early_buffer(HID // P, SEQ)
        simT = early_buffer(HALVES, SEQ)
        attnT = sb("attnT", [P, HALVES, SEQ])
        gatedT = early_buffer(HID // P, SEQ)

        u_var = sb("u_var", [P, HALVES])
        u_neg = sb("u_neg", [P, HALVES])
        u_scale = sb("u_scale", [P, HALVES])
        u_bias = sb("u_bias", [P, HALVES])
        row_a = sb("row_a", [P, HALVES, ROW])
        row_b = sb("row_b", [P, HALVES, ROW])
        u_sb = xsq
        uT = coef[0:KC, :, 0:SEQ]
        logitsT = sb("logitsT", [EXPERTS, SEQ])
        before_bf = sb("before_bf", [P, P], bf16)
        ones_bf = sb("ones_bf", [P, P], bf16)
        logits = sb("logits", [P, HALVES, EXPERTS])
        above = sb("above", [P, HALVES, EXPERTS, EXPERTS])
        equal = sb("equal", [P, HALVES, EXPERTS, EXPERTS])
        rank = sb("rank", [P, HALVES, EXPERTS])
        chosen = sb("chosen", [P, 2, HALVES * EXPERTS])
        in_row = sb("in_row", [P, EXPERTS], bf16)
        in_first = sb("in_first", [P, EXPERTS])
        picked = sb("picked", [P, 2, HALVES * EXPERTS])
        top = sb("top", [P, 2, HALVES])
        diff = sb("diff", [P, HALVES])
        tanh_d = sb("tanh_d", [P, HALVES])
        list_at = sb("list_at", [P, EXPERTS])
        slot = sb("slot", [P, HALVES, EXPERTS])
        slots = sb("slots", [P, 2, HALVES], i32)
        pad_rows = sb("pad_rows", [P, ROW])

        n_list = sb("n_list", [P, EXPERTS])
        over = sb("over", [P, EXPERTS, TOKENS // P])
        n_tiles = sb("n_tiles", [P, EXPERTS])
        t_end = sb("t_end", [P, EXPERTS])
        t_start = sb("t_start", [P, EXPERTS])
        base = sb("base", [P, EXPERTS])
        started = sb("started", [P, EXPERTS])
        used = sb("used", [P, 2, EXPERTS])
        list_earlier = sb("list_earlier", [P, EXPERTS])
        list_first = sb("list_first", [P, EXPERTS])
        table_parts = sb("table_parts", [P, 2, EXPERTS])
        table = sb("table", [P, 2])
        tile_expert = sb("tile_expert", [1, MOE_TILES], i32)
        tile_row = sb("tile_row", [1, MOE_TILES], i32)
        list_end = sb("list_end", [P, EXPERTS], i32)

        w_hi = sb("w_hi", [KC + 1, NSLICE, SLICE], f32r)
        w_lo = sb("w_lo", [KC + 1, NSLICE, SLICE], f32r)
        w_hid_parts = (w_hi[:, 0:NKC, :], w_lo[:, 0:NKC, :])
        w_i_parts = [w[:, NKC:NSLICE, :].rearrange("p (e b) f -> p e (b f)", e=EXPERTS) for w in (w_hi, w_lo)]
        b_o_sb = sb("b_o_sb", [P, EXPERTS, D])
        slot_rows = sb("slot_rows", [P, 2, ROW])
        meta = sb("meta", [P, MOE_TILES, 2], i32)
        sT_hi = sb("sT_hi", [KC + 1, NKC, P], f32r)
        sT_lo = sb("sT_lo", [KC + 1, NKC, P], f32r)
        h_sb = sb("h_sb", [P, FF])
        hT = sb("hT", [P, FF])
        stages = [t[0:KC + 1, :] for t in (h_sb, hT)]
        y_sb = sb("y_sb", [P, D])
        y_id = sb("y_id", [P, 1], i32)

        ps = ctx.enter_context(nc.psum_tensor("ps", [P, 8, 512], f32))

        ps_coef = ps[0:KC, 0:2, 0:NFC * FCH]
        ps_mix = ps[:, 2:4, :].rearrange("p b (k c) -> p (b k) c", c=256)[0:FCH, 0:NFC, 0:D]
        ps_conv = ps[:, 4, 0:HALVES * D].rearrange("p (t c) -> p t c", c=D)
        ps_gsum, ps_gsq = ps[:, 5, 0:GROUPS], ps[:, 6, 0:GROUPS]
        ps_nT = ps[0:KC, 0, :].rearrange("p (k n) -> p k n", k=NKC)
        ps_z = ps[0:QK, 1, 0:SEQ]
        ps_sim = ps[:, 1, :].rearrange("p (t n) -> p t n", t=HALVES)
        ps_v = ps[:, 2:4, 0:HID]
        ps_av = ps[:, 2:4, :].rearrange("p b (k n) -> p (b k) n", n=SEQ)[:, 0:HID // P, :]
        ps_gate = ps[:, 4:6, :].rearrange("p b (k n) -> p (b k) n", n=SEQ)[:, 0:HID // P, :]
        ps_out = ps[:, 6, 0:HALVES * D].rearrange("p (t c) -> p t c", c=D)
        ps_uT = ps[0:KC, 7, :].rearrange("p (k n) -> p k n", k=NKC)
        ps_logitsT = ps[0:EXPERTS, 7, 0:SEQ]
        ps_logits = ps[:, 7, SEQ:SEQ + HALVES * EXPERTS].rearrange("p (t e) -> p t e", e=EXPERTS)
        ps_rows_before = ps[:, 7, 384:384 + EXPERTS]
        ps_rows_all = ps[:, 7, 448:448 + EXPERTS]
        ps_table = ps[0:1, 6, 0:2 * P]
        ps_h = ps[:, 0:2, 0:FF // 2]
        ps_hT = ps[:, 2:4, 0:FF // 2]
        ps_sT = ps[0:KC, 4, 0:NKC * P].rearrange("p (k n) -> p k n", k=NKC)
        ps_y = ps[:, 5, 0:D]

        ld_const, ld_rest, ld_w1, ld_attn, ld_exp = (sem(f"ld_{n}") for n in ("const", "rest", "w1", "attn", "exp"))
        ld_x = [sem(f"ld_x{n}") for n in range(len(X_GROUPS))]
        stage_in = [sem(f"stage_in_{n}") for n in ("even", "odd")]
        hi_done, parts_done = sem("hi_done"), sem("parts_done")
        qk_hi_done, qk_parts_done = sem("qk_hi_done"), sem("qk_parts_done")
        nT_full_done, nT_hi_done = sem("nT_full_done"), sem("nT_hi_done")
        bf_set = sem("bf_set")
        ones_set = sem("ones_set")
        dve_self, pool_self = sem("dve_self"), sem("pool_self")
        gsum_in, gsum_done = sem("gsum_in"), sem("gsum_done")
        xc_done, sq_done = sem("xc_done"), sem("sq_done")
        gsq_in, gsq_done, grs_done, xn_done = sem("gsq_in"), sem("gsq_done"), sem("grs_done"), sem("xn_done")
        gmean_done = sem("gmean_done")
        coef_ps, coef_done = sem("coef_ps"), sem("coef_done")
        mix_ps, mix_done, conv_ps, conv_read = (
            sem(n) for n in ("mix_ps", "mix_done", "conv_ps", "conv_read"))
        scales_done = sem("scales_done")
        normed_done, nT_ps, nT_done, z_ps, z_done, qk_done = (
            sem(n) for n in ("normed_done", "nT_ps", "nT_done", "z_ps", "z_done", "qk_done"))
        v_ps, v_done, sim_ps, sim_done, attn_done, gate_ps, gate_done = (
            sem(n) for n in ("v_ps", "v_done", "sim_ps", "sim_done", "attn_done", "gate_ps", "gate_done"))
        av_ps, gated_done, out_ps, base_done, t2_done = (
            sem(n) for n in ("av_ps", "gated_done", "out_ps", "base_done", "t2_done"))
        weights_done, uT_ps, uT_done = sem("weights_done"), sem("uT_ps"), sem("uT_done")
        logits_ps, in_row_done, prefix_ps, prefix_read, diff_done, tanh_done, slots_done = (
            sem(n) for n in ("logits_ps", "in_row_done", "prefix_ps", "prefix_read", "diff_done", "tanh_done",
                             "slots_done"))
        ids_a_done, ids_b_done, scattered = sem("ids_a_done"), sem("ids_b_done"), sem("scattered")
        u_rows_done, sum_done = sem("u_rows_done"), sem("sum_done")
        stored, padded = sem("stored"), sem("padded")
        copies_done, logitsT_ps, logitsT_done = sem("copies_done"), sem("logitsT_ps"), sem("logitsT_done")
        tiles_done, pads_ready = sem("tiles_done"), sem("pads_ready")
        sT_hi_done = sem("sT_hi_done")
        ends_done, table_in, table_ps = sem("ends_done"), sem("table_in"), sem("table_ps")
        rows_in = [sem(f"rows_in_{n}") for n in ("even", "odd")]
        sT_ps, sT_done, meta_done, h_ps, h_done, hT_ps, hT_done, y_ps, y_read, y_done, added = (
            sem(n) for n in ("sT_ps", "sT_done", "meta_done", "h_ps", "h_done", "hT_ps", "hT_done",
                             "y_ps", "y_read", "y_done", "added"))

        block = ctx.enter_context(nc.Block())

        CONV = dict(first=-4, last=IMAGES, ahead=4, behind=1, unroll=2, parity=True)
        ATTN = dict(first=-1, last=IMAGES + 1, ahead=1, behind=2, unroll=2)
        MOE = dict(first=-1, last=MOE_TILES, ahead=1, behind=1, unroll=2, parity=True)

        def absent(i, n=IMAGES):
            return isinstance(i, int) and not 0 <= i < n

        def under_conv(i):
            return isinstance(i, int) and i == 0

        def tiles(i):
            return ds(i * HALVES, HALVES)

        def grouped(ap):
            return ap.rearrange("p t (g c) -> p t g c", c=GC)

        def over_channels(ap):
            return ap.unsqueeze(1).unsqueeze(3).broadcast_to((P, HALVES, GROUPS, GC))

        def pad_lists(eng, experts):
            eng.wait_ge(ends_done, 1)
            for e in experts:
                at = eng.value_load(list_end[0:1, e:e + 1], min_val=e * REGION, max_val=e * REGION + TOKENS)
                eng.dma_start(lists[ds(at, P), :], pad_rows[:, :]).then_inc(padded, 16)

        @block.sync
        def _(sp):
            def load_slice(n, odd):
                sp.dma_start(stages[odd].unsqueeze(1), split_w[:, ds(n, 1), :]).then_inc(stage_in[odd], 16)

            xv = x.rearrange("(n p) c -> p n c", p=P)
            split = CONST_AT["ones"][1]
            sp.dma_start(const[:, 0:split], consts[:, 0:split]).then_inc(ld_const, 16)
            first = 0
            for n, (group, images) in enumerate(zip(ld_x, X_GROUPS)):
                here = slice(first * HALVES, (first + images) * HALVES)
                sp.dma_start(X[:, here, :], xv[:, here, :]).then_inc(group, 16)
                first += images
                if n == 1:
                    sp.dma_start(const[:, split:], consts[:, split:]).then_inc(ld_rest, 16)
                if n == 2:
                    for odd in range(2):
                        load_slice(odd, odd)
            sp.dma_start(w_qk_sb[:, :, :], w_qk).then_inc(ld_attn, 16)
            sp.dma_start(w_out_sb[:, :, :], w_out).then_inc(ld_attn, 16)
            sp.dma_start(ln_sb[:, 0, :], ln_w).then_inc(ld_attn, 16)
            sp.dma_start(ln_sb[:, 1, :], ln_b).then_inc(ld_attn, 16)
            sp.dma_start(gb_sb[:, 0:2], gamma).then_inc(ld_attn, 16)
            sp.dma_start(gb_sb[:, 2:4], beta).then_inc(ld_attn, 16)
            sp.dma_start(b_out_sb[:, :], b_out.partition_broadcast(P)).then_inc(ld_attn, 16)
            sp.dma_start(w_r_sb[:, :, :], w_r).then_inc(ld_attn, 16)
            sp.dma_start(b_o_sb[:, :, :], b_o.partition_broadcast(P)).then_inc(ld_attn, 16)

            with sp.Fori(2, NSLICE - 1, 2) as n:
                for odd in range(2):
                    wait_alone(sp, parts_done, n + odd - 1, ld_const)
                    load_slice(n + odd, odd)

            sp.wait_ge(pads_ready, 1)
            sp.dma_start(out[TOKENS:TOKENS + P, :], pad_rows[:, 0:D]).then_inc(stored, 16)
            sp.dma_start(lists[SPARE:SPARE + P, :], pad_rows[:, :]).then_inc(padded, 16)

            ov = out[0:TOKENS, :].rearrange("(n p) c -> p n c", p=P)
            def store(i):
                wait_alone(sp, t2_done, i + 1, ld_const)
                sp.dma_start(ov[:, tiles(i), :], X[:, tiles(i), :]).then_inc(stored, 16)

            with sp.Fori(0, LOADED_EARLY) as e:
                for n in range(SHARED):
                    store(e * SHARED + n)
                sp.wait_ge(stored, e * (16 * SHARED) + 16 * (SHARED + 1))
                wait_alone(sp, u_rows_done, e * SHARED + SHARED, ld_const)
                sp.dma_start(w_o_sb[:, ds(e, 1), :, :], w_o[:, ds(e, 1), :, :]).then_inc(ld_exp, 16)
            for i in range(LOADED_EARLY * SHARED, IMAGES):
                store(i)

            def load_tile(j, odd):
                at = sp.value_load(tile_row[0:1, ds(j, 1)], min_val=0, max_val=SPARE)
                sp.dma_start(slot_rows[:, odd, :], lists[ds(at, P), :]).then_inc(rows_in[odd], 16)

            sp.wait_ge(tiles_done, 2)
            sp.wait_ge(scattered, 16 * 2 * HALVES * (IMAGES - 2))
            for j in range(2):
                load_tile(j, j)
            sp.wait_ge(stored, 16 * (IMAGES + 1))
            sp.wait_ge(u_rows_done, IMAGES)
            for e in range(LOADED_EARLY, EXPERTS):
                sp.dma_start(w_o_sb[:, e, :, :], w_o[:, e, :, :]).then_inc(ld_exp, 16)
            pad_lists(sp, range(EXPERTS // 2))

            def load_next(j, odd):
                wait_alone(sp, sT_ps, j - 1, ld_const)
                sp.wait_ge(meta_done, j - 1)
                load_tile(j, odd)

            for j in range(2, FIRST_TILES):
                load_next(j, j % 2)
            sp.wait_ge(tiles_done, 4)
            sp.wait_ge(padded, 16 * (EXPERTS + 1))
            sp.wait_ge(scattered, 16 * 2 * HALVES * IMAGES)
            load_next(FIRST_TILES, FIRST_TILES % 2)
            with sp.Fori(FIRST_TILES + 1, MOE_TILES - 1, 2) as j:
                for odd in range(2):
                    load_next(j + odd, odd)
            load_next(MOE_TILES - 1, 0)

        @block.gpsimd
        def _(pool):
            chain = Chain(pool, pool_self)
            last_rows = ((coef[KC:KC + 1, NKC - 1, :], 1.0),
                         (nT_hi[KC:KC + 1, NKC - 1, :].bitcast(f32), 1.0),
                         (nT_lo[KC:KC + 1, NKC - 1, :].bitcast(f32), 0.0),
                         (sT_hi[KC:KC + 1, NKC - 1, :].bitcast(f32), 1.0),
                         (sT_lo[KC:KC + 1, NKC - 1, :].bitcast(f32), 0.0))
            for n, (dst, value) in enumerate(last_rows):
                pool.memset(dst, value).then_inc(ones_set, 1)
                pool.wait_ge(ones_set, n + 1)
            pool.wait_ge(ld_const, 16)

            def set_up_lists():
                chain.link(pool.memset(pad_rows[:, :], 0.0))
                pool.wait_ge(ld_rest, 16)
                chain.link(pool.tensor_copy(pad_rows[:, D:D + 1].bitcast(i32), K("pad_id")))
                pool.tensor_copy(list_at[:, :], K("list_base")).then_inc(pads_ready, 1)
                for rows in (row_a, row_b):
                    chain.link(pool.tensor_copy(rows[:, :, D:D + 1].bitcast(i32), K("ids").unsqueeze(2)))
                chain.link(pool.tensor_copy(before_bf[:, :], K("before")))
                pool.tensor_copy(ones_bf[:, :], K("ones")).then_inc(bf_set, 1)
                pool.wait_ge(bf_set, 1)

            def conv_step(i, odd):
                if isinstance(i, int) and i == IMAGES - 2:
                    set_up_lists()
                if not absent(i + 3):
                    wait(pool, xn_done, i + 2)
                    wait(pool, sq_done, i + 2)
                    wait_alone(pool, gmean_done, i + 4, ld_const)
                    pool.tensor_tensor(grouped(xc[:, 1 - odd, :, :]), grouped(X[:, tiles(i + 3), :]),
                                       over_channels(gmean[:, :]), ALU.subtract).then_inc(xc_done, 1)
                if not absent(i + 1, NSLICE):
                    n = i + 1
                    wait_alone(pool, hi_done, n + 1, ld_const)
                    pool.tensor_tensor(w_lo[:, ds(n, 1), :], stages[1 - odd].unsqueeze(1),
                                       w_hi[:, ds(n, 1), :].bitcast(f32), ALU.subtract).then_inc(parts_done, 1)
                if not absent(i + 2):
                    wait_alone(pool, grs_done, i + 3, ld_const)
                    wait(pool, coef_ps, i + 2)
                    pool.tensor_tensor(grouped(xn[:, :, :]), grouped(xc[:, odd, :, :]),
                                       over_channels(grs[:, :]), ALU.mult).then_inc(xn_done, 1)
            pipeline(pool, conv_step, **CONV)

            def attn_step(i):
                r = i - 2
                if not absent(r):
                    pool.wait_ge(copies_done, r + 1)
                if not absent(i):
                    whole = X[:, tiles(i), :]
                    wait_alone(pool, sum_done, i + 1, ld_const)
                    pool.tensor_tensor(whole, whole, b_out_sb[:, :].unsqueeze(1).broadcast_to((P, HALVES, D)),
                                       ALU.add).then_inc(base_done, 1)
                if not absent(r):
                    for rows, ids_done in ((row_a, ids_a_done), (row_b, ids_b_done)):
                        ids = rows[:, :, D:D + 1].bitcast(i32)
                        pool.tensor_scalar(ids, ids, SEQ, None, ALU.add).then_inc(ids_done, 1)
                    wait_alone(pool, ids_a_done, r + 1, ld_const)
                    pool.wait_ge(ids_b_done, r + 1)
                    pool.wait_ge(weights_done, r + 1)
                    pool.wait_ge(slots_done, r + 1)
                    for c, rows in enumerate((row_a, row_b)):
                        for t in range(HALVES):
                            pool.indirect_dma_start(
                                out=lists, out_offset=bass.IndirectOffsetOnAxis(ap=slots[:, c, t:t + 1], axis=0),
                                in_=rows[:, t, :], in_offset=None).then_inc(scattered, 16)
                    pool.wait_ge(scattered, (r + 1) * (16 * 2 * HALVES))

            pool.wait_ge(ld_attn, 16 * 9)
            pool.wait_ge(qk_hi_done, 1)
            pool.tensor_tensor(w_qk_lo[:, :, :], w_qk_sb[:, :, :], w_qk_hi[:, :, :].bitcast(f32),
                               ALU.subtract).then_inc(qk_parts_done, 1)
            pipeline(pool, attn_step, **ATTN)

            pool.wait_ge(stored, 16 * (IMAGES + 1))
            with pool.Fori(1, MOE_TILES + 1) as n:
                wait_alone(pool, y_done, n, ld_const)
                pool.indirect_dma_start(out=out, out_offset=bass.IndirectOffsetOnAxis(ap=y_id[:, 0:1], axis=0),
                                        in_=y_sb[:, :], in_offset=None, compute_op=ALU.add).then_inc(added, 16)
                pool.wait_ge(added, n * 16)

        @block.scalar
        def _(act):
            act.dma_start(w1_sb[0:KC, :, :], w1).then_inc(ld_w1, 16)
            act.dma_start(w1_sb[KC:KC + 1, NKC - 1, :], b1).then_inc(ld_w1, 16)

            def normalise(i):
                wait(act, nT_ps, i)
                act.wait_ge(scales_done, 1 if isinstance(i, int) and i <= 2 else 2)
                for t in range(HALVES):
                    at = ds(i * HALVES + t, 1)
                    last = act.activation(normed[:, t, :].unsqueeze(1), X[:, at, :], ACT.Identity, bias=n_bias[:, at],
                                          scale=n_scale[:, at])
                last.then_inc(normed_done, 1)

            def conv_step(i, odd):
                if not absent(i + 3):
                    act.wait_ge(xc_done, i + 4)
                    wait(act, gsq_in, i + 3)
                    act.activation(xsq[:, :, :], xc[:, 1 - odd, :, :], ACT.Square).then_inc(sq_done, 1)
                if isinstance(i, int) and i == IMAGES - 1:
                    normalise(0)
                if not absent(i):
                    act.wait_ge(mix_ps, i + 1)
                    act.activation(mixed[:, :, :], ps_mix, ACT.Gelu).then_inc(mix_done, 1)
                if not absent(i + 1):
                    act.wait_ge(coef_ps, i + 2)
                    act.activation(coef[0:KC, :, :], ps_coef, ACT.Copy).then_inc(coef_done, 1)
                if not absent(i + 2, NSLICE):
                    n = i + 2
                    act.wait_ge(stage_in[odd], (n - odd + 2) * 8)
                    act.activation(w_hi[:, ds(n, 1), :], stages[odd].unsqueeze(1), ACT.Copy).then_inc(hi_done, 1)

            pipeline(act, conv_step, **CONV)

            act.wait_ge(ld_attn, 16 * 9)
            act.activation(w_qk_hi[:, :, :], w_qk_sb[:, :, :], ACT.Copy).then_inc(qk_hi_done, 1)

            def attn_step(i):
                r = i - 1
                if not absent(i + 1) and not under_conv(i + 1):
                    normalise(i + 1)
                if not absent(i):
                    act.wait_ge(normed_done, i + 1)
                    for t in range(HALVES):
                        at = ds(i * HALVES + t, 1)
                        last = act.activation(X[:, at, :], X[:, at, :], ACT.Identity, bias=r_bias[:, at],
                                              scale=r_scale[:, at])
                    last.then_inc(sum_done, 1)
                if not absent(i):
                    act.wait_ge(v_ps, i + 1)
                    act.activation(v_sb[:, :, :], ps_v, ACT.Silu).then_inc(v_done, 1)
                if not absent(i):
                    act.wait_ge(sim_ps, i + 1)
                    act.activation(simT[:, :, :], ps_sim, ACT.Relu, scale=1.0 / SEQ).then_inc(sim_done, 1)
                    act.wait_ge(sim_done, i + 1)
                    act.activation(attnT[:, :, :], simT[:, :, :], ACT.Square).then_inc(attn_done, 1)
                if not absent(i - 2):
                    act.wait_ge(diff_done, i - 1)
                    act.activation(tanh_d[:, :], diff[:, :], ACT.Tanh, scale=0.5).then_inc(tanh_done, 1)
                    wait(act, scattered, (i - 2) * (16 * 2 * HALVES))
                    act.wait_ge(u_rows_done, i - 1)
                    act.activation(row_a[:, :, 0:D], u_sb[:, :, :], ACT.Copy)
                    act.activation(row_b[:, :, 0:D], u_sb[:, :, :], ACT.Copy).then_inc(copies_done, 1)
                if not absent(i):
                    act.wait_ge(gate_ps, i + 1)
                    act.activation(gateT[:, :, :], ps_gate, ACT.Silu).then_inc(gate_done, 1)
                if not absent(i + 1):
                    act.wait_ge(nT_ps, i + 2)
                    wait(act, nT_done, i + 1)
                    for dst, done in ((nT, nT_full_done), (nT_hi, nT_hi_done)):
                        for k in range(NKC):
                            last = act.activation(dst[0:KC, k, :], ps_nT[:, k, :], ACT.Identity,
                                                  bias=ln_sb[:, 1, k:k + 1], scale=ln_sb[:, 0, k:k + 1])
                        last.then_inc(done, 1)
                if not absent(r):
                    act.wait_ge(uT_ps, r + 1)
                    act.activation(uT[:, :, :], ps_uT, ACT.Copy).then_inc(uT_done, 1)
                    act.wait_ge(logitsT_ps, r + 1)
                    act.activation(logitsT[:, :], ps_logitsT, ACT.Copy).then_inc(logitsT_done, 1)
                if not absent(i + 1):
                    act.wait_ge(z_ps, i + 2)
                    act.activation(zT[:, :], ps_z, ACT.Silu).then_inc(z_done, 1)

            pipeline(act, attn_step, **ATTN)

            pad_lists(act, range(EXPERTS // 2, EXPERTS))
            with act.Fori(0, MOE_TILES) as j:
                act.wait_ge(h_ps, j + 1)
                act.activation(h_sb[:, :].rearrange("p (b n) -> p b n", b=2), ps_h, ACT.Gelu).then_inc(h_done, 1)

            act.wait_ge(added, 16 * MOE_TILES)
            act.wait_ge(stored, 16 * (IMAGES + 1))

        @block.vector
        def _(dve):
            chain = Chain(dve, dve_self)
            INV_GROUP = 1.0 / (SEQ * GC)

            def token_moments(i):
                for t in range(HALVES):
                    last = dve.bn_stats(stats[:, t, :], X[:, ds(i * HALVES + t, 1), :])
                dve.drain()
                for t in range(HALVES):
                    last = dve.bn_aggr(mom[:, t, :], stats[:, t, :])
                chain.link(last)

            def rsqrt(y, v, neg_half_v, work):
                chain.link(dve.tensor_scalar(y.bitcast(i32), v.bitcast(i32), -0.5, float(0x5F3759DF),
                                             ALU.mult, ALU.add))
                for n in range(3):
                    chain.link(dve.tensor_tensor(work, neg_half_v, y, ALU.mult))
                    chain.link(dve.tensor_tensor(work, work, y, ALU.mult))
                    last = dve.scalar_tensor_tensor(y, work, 1.5, y, ALU.add, ALU.mult)
                    if n < 2:
                        chain.link(last)
                return last

            def conv_step(i, odd):
                if not absent(i + 3):
                    dve.wait_ge(gsum_done, i + 4)
                    wait(dve, xc_done, i + 3)
                    dve.tensor_scalar(gmean[:, :], ps_gsum, INV_GROUP, None, ALU.mult).then_inc(gmean_done, 1)
                if not absent(i - 1):
                    dve.wait_ge(conv_ps, i)
                    dve.tensor_tensor(X[:, tiles(i - 1), :], X[:, tiles(i - 1), :], ps_conv,
                                      ALU.add).then_inc(conv_read, 1)
                if not absent(i + 2):
                    dve.wait_ge(gsq_done, i + 3)
                    dve.tensor_scalar(gneg[:, :], ps_gsq, -0.5 * INV_GROUP, -0.5 * LN_EPS, ALU.mult, ALU.add)
                    chain.link(dve.tensor_scalar(gvar[:, :], ps_gsq, INV_GROUP, LN_EPS, ALU.mult, ALU.add))
                    wait(dve, xn_done, i + 2)
                    chain.mark(dve.tensor_scalar(grs[:, :].bitcast(i32), gvar[:, :].bitcast(i32), -0.5,
                                                 float(0x5F3759DF), ALU.mult, ALU.add))
                if not absent(i - 1):
                    wait_alone(dve, conv_read, i, ld_const)
                    dve.bn_stats(stats[:, 0, :], X[:, ds((i - 1) * HALVES, 1), :])
                if not absent(i + 2):
                    chain.wait()
                    chain.mark(dve.tensor_tensor(newton[:, :], gneg[:, :], grs[:, :], ALU.mult))
                if not absent(i - 1):
                    dve.bn_stats(stats[:, 1, :], X[:, ds((i - 1) * HALVES + 1, 1), :])
                if not absent(i + 2):
                    chain.wait()
                    chain.mark(dve.tensor_tensor(newton[:, :], newton[:, :], grs[:, :], ALU.mult))
                if not absent(i + 4):
                    first = 0
                    for group, images in zip(ld_x, X_GROUPS):
                        if not isinstance(i, int) or first <= i + 4 < first + images:
                            dve.wait_ge(group, 16)
                        first += images
                    wait(dve, gsum_done, i + 4)
                    dve.tensor_reduce(gsum[:, :], grouped(X[:, tiles(i + 4), :]).rearrange("p t g c -> p g t c"),
                                      AX.XY, ALU.add).then_inc(gsum_in, 1)
                if not absent(i + 2):
                    chain.wait()
                    chain.mark(dve.scalar_tensor_tensor(grs[:, :], newton[:, :], 1.5, grs[:, :], ALU.add, ALU.mult))
                if not absent(i - 1):
                    dve.drain()
                    for t in range(HALVES):
                        last = dve.bn_aggr(mom[:, t, :], stats[:, t, :])
                    chain.mark(last)
                if not absent(i + 2):
                    chain.wait()
                    chain.mark(dve.tensor_tensor(newton[:, :], gneg[:, :], grs[:, :], ALU.mult))
                if not absent(i - 1):
                    chain.wait()
                    chain.mark(dve.tensor_copy(moments[:, tiles(i - 1), :], mom[:, :, :]))
                if not absent(i + 2):
                    chain.wait()
                    chain.link(dve.tensor_tensor(newton[:, :], newton[:, :], grs[:, :], ALU.mult))
                    chain.mark(dve.scalar_tensor_tensor(grs[:, :], newton[:, :], 1.5, grs[:, :], ALU.add, ALU.mult))
                if not absent(i + 3):
                    dve.wait_ge(sq_done, i + 4)
                    wait(dve, gsq_done, i + 3)
                    dve.tensor_reduce(gsq[:, :], grouped(xsq[:, :, :]).rearrange("p t g c -> p g t c"),
                                      AX.XY, ALU.add).then_inc(gsq_in, 1)
                if not absent(i + 2):
                    chain.wait()
                    chain.link(dve.tensor_tensor(newton[:, :], gneg[:, :], grs[:, :], ALU.mult))
                    chain.link(dve.tensor_tensor(newton[:, :], newton[:, :], grs[:, :], ALU.mult))
                    dve.scalar_tensor_tensor(grs[:, :], newton[:, :], 1.5, grs[:, :], ALU.add,
                                             ALU.mult).then_inc(grs_done, 1)
                elif not absent(i - 1):
                    chain.wait()

            def first_scales(lo, hi):
                mean, var, rs = moments[:, lo:hi, 0], moments[:, lo:hi, 1], rs1[:, lo:hi]
                v, neg, work = ln_var[:, lo:hi], ln_neg[:, lo:hi], ln_work[:, lo:hi]
                dve.tensor_scalar(neg, var, -0.5, -0.5 * LN_EPS, ALU.mult, ALU.add)
                chain.link(dve.tensor_scalar(v, var, LN_EPS, None, ALU.add))
                chain.link(rsqrt(rs, v, neg, work))
                dve.tensor_scalar(r_scale[:, lo:hi], rs, 1.0, None, ALU.add)
                dve.scalar_tensor_tensor(r_bias[:, lo:hi], mean, -1.0, rs, ALU.mult, ALU.mult)

            def second_scales(lo, hi):
                mean, var, rs = moments[:, lo:hi, 0], moments[:, lo:hi, 1], rs1[:, lo:hi]
                v, neg, work = ln_var[:, lo:hi], ln_neg[:, lo:hi], ln_work[:, lo:hi]
                ns, nb = n_scale[:, lo:hi], n_bias[:, lo:hi]
                chain.link(dve.tensor_tensor(work, var, rs, ALU.mult))
                chain.link(dve.tensor_tensor(work, work, rs, ALU.mult))
                dve.tensor_scalar(neg, work, -0.5, -0.5 * LN_EPS, ALU.mult, ALU.add)
                chain.link(dve.tensor_scalar(v, work, LN_EPS, None, ALU.add))
                chain.link(rsqrt(ns, v, neg, work))
                chain.link(dve.tensor_tensor(ns, ns, rs, ALU.mult))
                dve.scalar_tensor_tensor(nb, mean, -1.0, ns, ALU.mult, ALU.mult).then_inc(scales_done, 1)

            def conv_or_scales(i, odd):
                conv_step(i, odd)
                if isinstance(i, int) and i == SCALED:
                    first_scales(0, SCALED * HALVES)
                if isinstance(i, int) and i == SCALED + 1:
                    second_scales(0, SCALED * HALVES)

            pipeline(dve, conv_or_scales, **CONV, chain=chain, per=12)

            def query_key(i):
                dve.wait_ge(z_done, i + 1)
                for n, dst in enumerate((qT, kT)):
                    last = dve.tensor_scalar(dst[:, :], zT[:, :], gb_sb[:, n:n + 1], gb_sb[:, 2 + n:3 + n],
                                             ALU.mult, ALU.add)
                last.then_inc(qk_done, 1)

            def choose(r):
                dve.wait_ge(logits_ps, r + 1)
                chain.link(dve.tensor_copy(logits[:, :, :], ps_logits))
                shape = (P, HALVES, EXPERTS, EXPERTS)
                other = logits[:, :, :].unsqueeze(2).broadcast_to(shape)
                own = logits[:, :, :].unsqueeze(3).broadcast_to(shape)
                dve.tensor_tensor(above[:, :, :, :], other, own, ALU.is_gt)
                chain.link(dve.tensor_tensor(equal[:, :, :, :], other, own, ALU.is_equal))
                lower = K("lower").rearrange("p (a b) -> p a b", b=EXPERTS).unsqueeze(1).broadcast_to(shape)
                chain.link(dve.tensor_tensor(equal[:, :, :, :], equal[:, :, :, :], lower, ALU.mult))
                chain.link(dve.tensor_tensor(above[:, :, :, :], above[:, :, :, :], equal[:, :, :, :], ALU.add))
                chain.link(dve.tensor_reduce(rank[:, :, :], above[:, :, :, :], AX.X, ALU.add))
                for c in range(2):
                    last = dve.tensor_scalar(chosen[:, c, :], rank[:, :, :].rearrange("p t e -> p (t e)"),
                                             float(c), None, ALU.is_equal)
                chain.link(last)
                by_expert = chosen[:, :, :].rearrange("p c (t e) -> p e c t", e=EXPERTS)
                with nc.allow_low_precision(reason="whole numbers up to 2"):
                    dve.tensor_reduce(in_row[:, :], by_expert, AX.XY, ALU.add).then_inc(in_row_done, 1)
                dve.tensor_tensor(in_first[:, :], chosen[:, 0, 0:EXPERTS], chosen[:, 1, 0:EXPERTS], ALU.add)
                both = logits[:, :, :].rearrange("p t e -> p (t e)").unsqueeze(1).broadcast_to(
                    (P, 2, HALVES * EXPERTS))
                chain.link(dve.tensor_tensor(picked[:, :, :], chosen[:, :, :], both, ALU.mult))
                chain.link(dve.tensor_reduce(top[:, :, :], picked[:, :, :].rearrange(
                    "p c (t e) -> p c t e", e=EXPERTS), AX.X, ALU.add))
                dve.tensor_tensor(diff[:, :], top[:, 0, :], top[:, 1, :], ALU.subtract).then_inc(diff_done, 1)

            def count(r):
                dve.wait_ge(prefix_ps, r + 1)
                chain.link(dve.tensor_tensor(slot[:, 0, :], list_at[:, :], ps_rows_before, ALU.add))
                dve.tensor_tensor(slot[:, 1, :], slot[:, 0, :], in_first[:, :], ALU.add)
                dve.tensor_tensor(list_at[:, :], list_at[:, :], ps_rows_all, ALU.add).then_inc(prefix_read, 1)

            def place(r):
                wait_alone(dve, prefix_read, r + 1, ld_const)
                wait(dve, scattered, r * (16 * 2 * HALVES))
                both = slot[:, :, :].rearrange("p t e -> p (t e)").unsqueeze(1).broadcast_to(
                    (P, 2, HALVES * EXPERTS))
                chain.link(dve.tensor_tensor(picked[:, :, :], chosen[:, :, :], both, ALU.mult))
                with nc.allow_low_precision(reason="whole numbers below 2**24"):
                    dve.tensor_reduce(slots[:, :, :], picked[:, :, :].rearrange("p c (t e) -> p c t e", e=EXPERTS),
                                      AX.X, ALU.add).then_inc(slots_done, 1)
                dve.wait_ge(tanh_done, r + 1)
                for rows, sign in ((row_a, 0.5), (row_b, -0.5)):
                    last = dve.tensor_scalar(rows[:, :, D + 1:D + 2], tanh_d[:, :].unsqueeze(2), sign, 0.5,
                                             ALU.mult, ALU.add)
                last.then_inc(weights_done, 1)

            def make_table(ends, firsts, rows_short, before):
                n_regions = (P, EXPERTS, TOKENS // P)
                chain.link(dve.tensor_tensor(n_list[:, :], ends, firsts, ALU.subtract))
                if rows_short:
                    chain.link(dve.tensor_scalar(n_list[:, :], n_list[:, :], -float(rows_short), None, ALU.add))
                chain.link(dve.tensor_tensor(over[:, :, :], n_list[:, :].unsqueeze(2).broadcast_to(n_regions),
                                             K("tile_rows").unsqueeze(1).broadcast_to(n_regions), ALU.is_gt))
                chain.link(dve.tensor_reduce(n_tiles[:, :], over[:, :, :], AX.X, ALU.add))
                chain.link(dve.tensor_tensor_scan(t_end[:, :], K("ones")[:, 0:EXPERTS], n_tiles[:, :],
                                                  float(before), ALU.mult, ALU.add))
                dve.tensor_scalar(table_parts[:, 1, :], t_end[:, :], K("tile_no"), None, ALU.is_le)
                chain.link(dve.tensor_tensor(t_start[:, :], t_end[:, :], n_tiles[:, :], ALU.subtract))
                dve.scalar_tensor_tensor(base[:, :], t_start[:, :], -float(P), firsts, ALU.mult, ALU.add)
                chain.link(dve.tensor_scalar(started[:, :], t_start[:, :], K("tile_no"), None, ALU.is_le))
                chain.link(dve.tensor_tensor(started[:, :], started[:, :], table_parts[:, 1, :], ALU.subtract))
                chain.link(dve.scalar_tensor_tensor(table_parts[:, 0, :], base[:, :], K("tile_at"), started[:, :],
                                                    ALU.add, ALU.mult))
                dve.tensor_reduce(table[:, :], table_parts[:, :, :], AX.X, ALU.add).then_inc(table_in, 1)

            def store_table(n, lo, hi):
                dve.wait_ge(table_ps, n)
                dve.tensor_scalar(tile_row[:, lo:hi], ps_table[:, lo:hi], float(SPARE), None,
                                  ALU.add).then_inc(tiles_done, 1)
                dve.tensor_scalar(tile_expert[:, lo:hi], ps_table[:, P + lo:P + hi], float(EXPERTS - 1), None,
                                  ALU.min).then_inc(tiles_done, 1)
                dve.wait_ge(tiles_done, 2 * n)

            def first_table():
                make_table(list_earlier[:, :], K("list_base"), P - 1, 0)
                dve.tensor_scalar(used[:, 0, :], t_start[:, :], float(FIRST_TILES), None, ALU.min)
                chain.link(dve.tensor_scalar(used[:, 1, :], t_end[:, :], float(FIRST_TILES), None, ALU.min))
                chain.link(dve.tensor_tensor(used[:, 0, :], used[:, 1, :], used[:, 0, :], ALU.subtract))
                chain.link(dve.scalar_tensor_tensor(list_first[:, :], used[:, 0, :], float(P), K("list_base"),
                                                    ALU.mult, ALU.add))
                store_table(1, 0, FIRST_TILES)

            def attn_step(i):
                r = i - 1
                if not absent(r):
                    wait(dve, uT_ps, r)
                    wait(dve, copies_done, r)
                    for t in range(HALVES):
                        last = dve.tensor_scalar(u_sb[:, t, :],
                                                 X[:, ds(r * HALVES + t, 1), :].rearrange("p a c -> p (a c)"),
                                                 u_scale[:, t:t + 1], u_bias[:, t:t + 1], ALU.mult, ALU.add)
                    last.then_inc(u_rows_done, 1)
                if isinstance(i, int) and i == IMAGES:
                    chain.link(dve.tensor_copy(list_earlier[:, :], list_at[:, :]))
                if not absent(i - 2):
                    count(i - 2)
                    place(i - 2)
                if isinstance(i, int) and i == IMAGES:
                    first_table()
                if isinstance(i, int) and i == 0:
                    first_scales(SCALED * HALVES, IMAGES * HALVES)
                    second_scales(SCALED * HALVES, IMAGES * HALVES)
                if not absent(i + 1):
                    wait_alone(dve, nT_hi_done, i + 2, ld_const)
                    dve.wait_ge(nT_full_done, i + 2)
                    dve.tensor_tensor(nT_lo[0:KC, :, :], nT[:, :, :], nT_hi[0:KC, :, :].bitcast(f32),
                                      ALU.subtract).then_inc(nT_done, 1)
                if not absent(i):
                    dve.wait_ge(gate_done, i + 1)
                    for k, (lo, hi) in enumerate(((0, 2), (2, 3))):
                        dve.wait_ge(av_ps, 2 * i + 1 + k)
                        dve.tensor_tensor(gatedT[:, lo:hi, :], ps_av[:, lo:hi, :], gateT[:, lo:hi, :],
                                          ALU.mult).then_inc(gated_done, 1)
                if not absent(i - 1):
                    choose(i - 1)
                if not absent(i + 1):
                    query_key(i + 1)
                if not absent(i):
                    dve.wait_ge(out_ps, i + 1)
                    dve.wait_ge(base_done, i + 1)
                    ins = dve.tensor_tensor(X[:, tiles(i), :], X[:, tiles(i), :], ps_out, ALU.add)
                    ins.then_inc(t2_done, 1)
                    wait_alone(dve, t2_done, i + 1, ld_const)
                    token_moments(i)
                    dve.tensor_scalar(u_neg[:, :], mom[:, :, 1], -0.5, -0.5 * LN_EPS, ALU.mult, ALU.add)
                    chain.link(dve.tensor_scalar(u_var[:, :], mom[:, :, 1], LN_EPS, None, ALU.add))
                    chain.link(rsqrt(u_scale[:, :], u_var[:, :], u_neg[:, :], newton[:, 0:HALVES]))
                    chain.link(dve.scalar_tensor_tensor(u_bias[:, :], mom[:, :, 0], -1.0, u_scale[:, :],
                                                        ALU.mult, ALU.mult))

            dve.wait_ge(ld_attn, 16 * 9)
            dve.wait_ge(pads_ready, 1)
            dve.wait_ge(ld_rest, 16)
            pipeline(dve, attn_step, **ATTN, chain=chain, per=23)

            dve.tensor_copy(list_end[:, :], list_at[:, :]).then_inc(ends_done, 1)

            def moe_step(j, odd):
                if not absent(j + 1, MOE_TILES):
                    dve.wait_ge(sT_ps, j + 2)
                    dve.tensor_copy(sT_hi[0:KC, :, :], ps_sT).then_inc(sT_hi_done, 1)
                    wait_alone(dve, sT_hi_done, j + 2, ld_const)
                    dve.tensor_tensor(sT_lo[0:KC, :, :], ps_sT, sT_hi[0:KC, :, :].bitcast(f32),
                                      ALU.subtract).then_inc(sT_done, 1)
                    dve.tensor_copy(meta[:, ds(j + 1, 1), :],
                                    slot_rows[:, 1 - odd, D:D + 2].bitcast(i32).unsqueeze(1)).then_inc(meta_done, 1)
                if isinstance(j, int) and j == -1:
                    make_table(list_at[:, :], list_first[:, :], 0, FIRST_TILES)
                if not absent(j - 1, MOE_TILES):
                    p = j - 1
                    e = dve.value_load(tile_expert[0:1, ds(p, 1)], min_val=0, max_val=EXPERTS - 1)
                    dve.wait_ge(y_ps, p + 1)
                    wait(dve, added, p * 16)
                    dve.tensor_tensor(y_sb[:, :].unsqueeze(1), ps_y.unsqueeze(1), b_o_sb[:, ds(e, 1), :],
                                      ALU.add).then_inc(y_read, 1)
                    dve.tensor_copy(y_id[:, :].unsqueeze(1), meta[:, ds(p, 1), 0:1])
                    dve.wait_ge(y_read, p + 1)
                    w = meta[:, ds(p, 1), 1:2].bitcast(f32)
                    dve.tensor_scalar(y_sb[:, :], y_sb[:, :], w.rearrange("p a b -> p (a b)"), None,
                                      ALU.mult).then_inc(y_done, 1)
                if not absent(j, MOE_TILES):
                    for k in range(2):
                        dve.wait_ge(hT_ps, 2 * j + 1 + k)
                        dve.tensor_copy(hT[:, k * FF // 2:(k + 1) * FF // 2], ps_hT[:, k, :]).then_inc(hT_done, 1)
                if isinstance(j, int) and j == 0:
                    store_table(2, FIRST_TILES, MOE_TILES)

            pipeline(dve, moe_step, **MOE)

        @block.tensor
        def _(pe):
            pe.wait_ge(ld_const, 16)
            pe.wait_ge(ones_set, 5)

            def mm(dst, lhsT, rhs, start=True, stop=True):
                return pe.matmul(dst, lhsT, rhs, start=start, stop=stop)

            def turn_table(n):
                pe.wait_ge(table_in, n)
                for c in range(2):
                    last = mm(ps_table[:, c * P:(c + 1) * P], table[:, c:c + 1], K("ident"))
                last.then_inc(table_ps, 1)

            def transpose_normed(i):
                pe.wait_ge(normed_done, i + 1)
                for t in range(HALVES):
                    for k in range(NKC):
                        last = pe.transpose(ps_nT[:, k, t * P:(t + 1) * P], normed[:, t, k * KC:(k + 1) * KC],
                                            K("ident"))
                last.then_inc(nT_ps, 1)

            def conv_step(i, odd):
                if not absent(i):
                    if isinstance(i, int) and i == 0:
                        pe.wait_ge(ld_w1, 32)
                    pe.wait_ge(coef_done, i + 1)
                    for f in range(NFC):
                        for k in range(NKC):
                            rows = KC + (k == NKC - 1)
                            last = mm(ps_mix[:, f, :], coef[0:rows, k, f * FCH:(f + 1) * FCH],
                                      w1_sb[0:rows, k, :], k == 0, k == NKC - 1)
                    last.then_inc(mix_ps, 1)
                if not absent(i + 1):
                    if isinstance(i, int) and i == -1:
                        pe.wait_ge(ld_rest, 16)
                    pe.wait_ge(xn_done, i + 2)
                    for k in range(NKC):
                        ch = slice(k * KC, (k + 1) * KC)
                        mm(ps_coef[:, k, 0:2 * FCH], xn[:, 0, ch], K("fwd0"), True, False)
                        mm(ps_coef[:, k, FCH:2 * FCH], xn[:, 1, ch], K("fwd1")[:, 0:FCH], False, True)
                        last = mm(ps_coef[:, k, 2 * FCH:3 * FCH], xn[:, 1, ch], K("fwd1")[:, FCH:2 * FCH])
                    last.then_inc(coef_ps, 1)
                if not absent(i + 4):
                    pe.wait_ge(gsum_in, i + 5)
                    wait(pe, gmean_done, i + 4)
                    mm(ps_gsum, K("ones"), gsum[:, :]).then_inc(gsum_done, 1)
                if isinstance(i, int) and i == IMAGES - 1:
                    transpose_normed(0)
                if not absent(i):
                    pe.wait_ge(mix_done, i + 1)
                    wait(pe, conv_read, i)
                    mm(ps_conv[:, 0, :], K("inv0a", FCH), mixed[:, 0, :], True, False)
                    mm(ps_conv[:, 0, :], K("inv0b", FCH), mixed[:, 1, :], False, True)
                    mm(ps_conv[:, 1, :], K("inv1b", FCH), mixed[:, 1, :], True, False)
                    mm(ps_conv[:, 1, :], K("inv1c", FCH), mixed[:, 2, :], False, True).then_inc(conv_ps, 1)
                if not absent(i + 3):
                    pe.wait_ge(gsq_in, i + 4)
                    wait(pe, grs_done, i + 3)
                    mm(ps_gsq, K("ones"), gsq[:, :]).then_inc(gsq_done, 1)

            pipeline(pe, conv_step, **CONV)
            pe.wait_ge(ld_attn, 16 * 9)
            pe.wait_ge(bf_set, 1)
            pe.wait_ge(qk_parts_done, 1)

            def split_mm(dst, lhsT, rhs, start, stop):
                (a_hi, a_lo), (b_hi, b_lo) = lhsT, rhs
                mm(dst, a_hi, b_hi, start, False)
                mm(dst, a_lo, b_hi, False, False)
                return mm(dst, a_hi, b_lo, False, stop)

            def z_product(i):
                pe.wait_ge(nT_done, i + 1)
                for k in range(NKC):
                    rows = KC + (k == NKC - 1)
                    last = split_mm(ps_z, [w[0:rows, k, :] for w in (w_qk_hi, w_qk_lo)],
                                    [n[0:rows, k, :] for n in (nT_hi, nT_lo)], k == 0, k == NKC - 1)
                last.then_inc(z_ps, 1)

            def gates(c):
                at = slice(HID + c * P, HID + (c + 1) * P)
                for k in range(NKC):
                    rows = KC + (k == NKC - 1)
                    last = split_mm(ps_gate[:, c, :], [w[0:rows, k, at] for w in w_hid_parts],
                                    [n[0:rows, k, :] for n in (nT_hi, nT_lo)], k == 0, k == NKC - 1)
                return last

            def attend(c):
                for t in range(HALVES):
                    last = mm(ps_av[:, c, :], v_sb[:, t, c * P:(c + 1) * P], attnT[:, t, :], t == 0, t == HALVES - 1)
                return last

            def attn_step(i):
                r = i - 1
                if not absent(i):
                    if isinstance(i, int) and i == 0:
                        pe.wait_ge(parts_done, NSLICE)
                    for t in range(HALVES):
                        for k in range(NKC):
                            rows = KC + (k == NKC - 1)
                            last = split_mm(ps_v[:, t, :], [n[0:rows, k, t * P:(t + 1) * P] for n in (nT_hi, nT_lo)],
                                            [w[0:rows, k, 0:HID] for w in w_hid_parts], k == 0, k == NKC - 1)
                    last.then_inc(v_ps, 1)
                if not absent(i):
                    pe.wait_ge(qk_done, i + 1)
                    for t in range(HALVES):
                        last = mm(ps_sim[:, t, :], kT[:, t * P:(t + 1) * P], qT[:, :])
                    last.then_inc(sim_ps, 1)
                if not absent(i - 2):
                    pe.wait_ge(in_row_done, i - 1)
                    mm(ps_rows_before, before_bf[:, :], in_row[:, :])
                    mm(ps_rows_all, ones_bf[:, :], in_row[:, :]).then_inc(prefix_ps, 1)
                if not absent(i):
                    gates(0)
                    gates(1)
                    gates(2).then_inc(gate_ps, 1)
                if not absent(i + 1) and not under_conv(i + 1):
                    transpose_normed(i + 1)
                if not absent(i):
                    pe.wait_ge(v_done, i + 1)
                    pe.wait_ge(attn_done, i + 1)
                    attend(0)
                    attend(1).then_inc(av_ps, 1)
                if not absent(r):
                    pe.wait_ge(u_rows_done, r + 1)
                    wait(pe, prefix_read, r)
                    for t in range(HALVES):
                        for k in range(NKC):
                            last = pe.transpose(ps_uT[:, k, t * P:(t + 1) * P], u_sb[:, t, k * KC:(k + 1) * KC],
                                                K("ident"))
                    last.then_inc(uT_ps, 1)
                if not absent(i):
                    attend(2).then_inc(av_ps, 1)
                if not absent(r):
                    pe.wait_ge(uT_done, r + 1)
                    for k in range(NKC):
                        last = mm(ps_logitsT, w_r_sb[:, k, :], uT[:, k, :], k == 0, k == NKC - 1)
                    last.then_inc(logitsT_ps, 1)
                if not absent(i + 1):
                    z_product(i + 1)
                if isinstance(i, int) and i == IMAGES:
                    turn_table(1)
                if not absent(r):
                    wait_alone(pe, logitsT_done, r + 1, ld_const)
                    for t in range(HALVES):
                        last = pe.transpose(ps_logits[:, t, :], logitsT[:, t * P:(t + 1) * P],
                                            K("ident", EXPERTS)[:, 0:EXPERTS])
                    last.then_inc(logits_ps, 1)
                if not absent(i):
                    wait(pe, t2_done, i)
                    pe.wait_ge(gated_done, 2 * i + 2)
                    for t in range(HALVES):
                        for c in range(HID // P):
                            last = mm(ps_out[:, t, :], gatedT[:, c, t * P:(t + 1) * P], w_out_sb[:, c, :],
                                      c == 0, c == HID // P - 1)
                    last.then_inc(out_ps, 1)

            pipeline(pe, attn_step, **ATTN)

            pe.wait_ge(tiles_done, 2)

            def moe_step(j, odd):
                if not absent(j, MOE_TILES):
                    e = pe.value_load(tile_expert[0:1, ds(j, 1)], min_val=0, max_val=EXPERTS - 1)
                    pe.wait_ge(sT_done, j + 1)
                    for b in range(2):
                        for k in range(NKC):
                            rows = KC + (k == NKC - 1)
                            at = (b * NKC + k) * HALF
                            last = split_mm(ps_h[:, b, :], [n[0:rows, k, :] for n in (sT_hi, sT_lo)],
                                            [w[0:rows, ds(e, 1), at:at + HALF] for w in w_i_parts],
                                            k == 0, k == NKC - 1)
                    last.then_inc(h_ps, 1)
                if not absent(j + 1, MOE_TILES):
                    pe.wait_ge(rows_in[1 - odd], (j + odd) * 8 + 16)
                    for k in range(NKC):
                        last = pe.transpose(ps_sT[:, k, :], slot_rows[:, 1 - odd, k * KC:(k + 1) * KC], K("ident"))
                    last.then_inc(sT_ps, 1)
                if not absent(j - 1, MOE_TILES):
                    p = j - 1
                    if isinstance(j, int) and j == 1:
                        pe.wait_ge(ld_exp, 16 * EXPERTS)
                        pe.wait_ge(tiles_done, 4)
                    e = pe.value_load(tile_expert[0:1, ds(p, 1)], min_val=0, max_val=EXPERTS - 1)
                    pe.wait_ge(hT_done, 2 * p + 2)
                    wait(pe, y_read, p)
                    for f in range(FCHUNKS):
                        last = mm(ps_y, hT[:, f * P:(f + 1) * P], w_o_sb[:, ds(e, 1), f, :], f == 0,
                                  f == FCHUNKS - 1)
                    last.then_inc(y_ps, 1)
                if not absent(j, MOE_TILES):
                    pe.wait_ge(h_done, j + 1)
                    for f in range(FCHUNKS):
                        b, c = divmod(f, FCHUNKS // 2)
                        last = pe.transpose(ps_hT[:, b, c * P:(c + 1) * P], h_sb[:, f * P:(f + 1) * P], K("ident"))
                        if c == FCHUNKS // 2 - 1:
                            last.then_inc(hT_ps, 1)
                if isinstance(j, int) and j == 0:
                    turn_table(2)

            pipeline(pe, moe_step, **MOE)


def kernel(x, L0_conv_W1, L0_conv_b1, L1_attn_ln_w, L1_attn_ln_b, L1_attn_W_hidden, L1_attn_b_hidden,
           L1_attn_W_qk, L1_attn_b_qk, L1_attn_gamma, L1_attn_beta, L1_attn_W_out, L1_attn_b_out,
           L1_ffn_Wr, L1_ffn_Wi, L1_ffn_bi, L1_ffn_Wo, L1_ffn_bo):
    import concourse.bacc as bacc
    from concourse.bass_utils import run_bass_kernel_spmd

    def packed(w, rows):
        w = np.asarray(w)
        w = w.reshape(*w.shape[:-1], w.shape[-1] // rows, rows)
        w = np.swapaxes(w, -3, -2)
        return np.ascontiguousarray(np.moveaxis(w, -1, 0))

    def columns(v):
        return np.ascontiguousarray(np.asarray(v).reshape(NKC, KC).T)

    def with_bias(w, b, columns):
        a = np.zeros((KC + 1, b.size // columns, NKC, columns), np.float32)
        a[0:KC] = w
        a[KC, :, NKC - 1] = b.reshape(-1, columns)
        return a

    b_hid, b_i, b_qk = (np.asarray(b) for b in (L1_attn_b_hidden, L1_ffn_bi, L1_attn_b_qk))
    w_i = packed(L1_ffn_Wi, KC).reshape(KC, EXPERTS, NKC, -1, HALF).swapaxes(2, 3).reshape(KC, -1, NKC, HALF)
    split_w = np.concatenate([with_bias(packed(L1_attn_W_hidden, KC)[:, None], b_hid, 2 * HID)[:, 0],
                              with_bias(w_i, b_i, HALF).reshape(KC + 1, -1, SLICE)], axis=1)

    arrays = {
        "x": np.asarray(x).reshape(TOKENS, D), "consts": shape_constants(),
        "w1": packed(L0_conv_W1, KC), "b1": np.asarray(L0_conv_b1).reshape(1, D),
        "ln_w": columns(L1_attn_ln_w), "ln_b": columns(L1_attn_ln_b),
        "split_w": split_w, "w_qk": with_bias(packed(L1_attn_W_qk, KC)[:, None], b_qk, QK)[:, 0],
        "gamma": np.ascontiguousarray(np.asarray(L1_attn_gamma).T),
        "beta": np.ascontiguousarray(np.asarray(L1_attn_beta).T),
        "w_out": packed(L1_attn_W_out, P), "b_out": np.asarray(L1_attn_b_out),
        "w_r": packed(L1_ffn_Wr, KC),
        "w_o": packed(L1_ffn_Wo, P), "b_o": np.asarray(L1_ffn_bo),
    }
    nc = bacc.Bacc("TRN2", target_bir_lowering=False, num_devices=1)
    aps = [nc.dram_tensor(f"in_{n}", a.shape, mybir.dt.from_np(a.dtype), kind="ExternalInput").ap()
           for n, a in arrays.items()]
    out = nc.dram_tensor("out_rows", (TOKENS + P, D), mybir.dt.float32, kind="ExternalOutput").ap()
    names = dict(zip(arrays, aps))
    build(nc, **names, out=out)
    r = run_bass_kernel_spmd(nc, [{f"in_{n}": a for n, a in arrays.items()}], core_ids=[0])
    return r.results[0]["out_rows"][:TOKENS].reshape(IMAGES, SIDE, SIDE, D)
```
